# Optimizing a Trainium2 kernel written in Bass

```python
import numpy as np
import jax
import jax.numpy as jnp

def _softmax(x, axis=-1):
    return jax.nn.softmax(x, axis=axis)

def _gelu(x):
    return jax.nn.gelu(x, approximate=True)

def _silu(x):
    return jax.nn.silu(x)

def _sigmoid(x):
    return jax.nn.sigmoid(x)

def _layernorm(x, axis=-1, eps=1e-05):
    m = jnp.mean(x, axis=axis, keepdims=True)
    v = jnp.var(x, axis=axis, keepdims=True)
    return (x - m) / jnp.sqrt(v + eps)

def _scatter_add(tgt, idx, src, axis=0):
    return tgt.at[idx].add(src)

def _segment_sum(src, seg, n):
    return jax.ops.segment_sum(src, seg, n)
kernel_name = 'mk_gnn_preln_d2_gnn_r8_2848f0'

def setup_inputs(seed: int=0):
    np.random.seed(seed)
    _w = jnp.asarray

    def _rec_inputs():
        import jax
        import jax.numpy as jnp
        _gk = jax.random.key(seed)
        x = -0.000202 + 1 * jax.random.normal(jax.random.fold_in(_gk, 1), (6250, 128), jnp.float32)
        src = jax.random.randint(jax.random.fold_in(_gk, 2), (100000,), 0, 6250, jnp.int32)
        dst = jnp.minimum((6250 * jax.random.uniform(jax.random.fold_in(_gk, 3), (100000,)) ** 2.0).astype(jnp.int32), 49999)
        _o = jnp.argsort(dst, stable=True)
        src = src[_o]
        dst = dst[_o]
        edge_weight = jax.random.uniform(jax.random.fold_in(_gk, 12), (100000,), jnp.float32, 0.0, 0.999998)
        return (x, src, dst, edge_weight)
    x, src, dst, edge_weight = _rec_inputs()

    def _L0_gnn_setup():
        import jax, jax.numpy as jnp
        import numpy as np
        N, E, D = (6250, 75000, 128)

        def gcn_conv(x, edge_index, edge_weight, W, b, num_nodes):
            row, col = (edge_index[0], edge_index[1])
            deg = jax.ops.segment_sum(edge_weight, col, num_segments=num_nodes)
            dis = jnp.where(deg > 0, jax.lax.rsqrt(jnp.where(deg > 0, deg, 1.0)), 0.0)
            norm = dis[row] * edge_weight * dis[col]
            xl = x @ W
            msg = xl[row] * norm[:, None]
            out = jax.ops.segment_sum(msg, col, num_segments=num_nodes)
            return out + b
        key = jax.random.key(seed)
        ks = jax.random.split(key, 7)
        x = jax.random.normal(ks[0], (N, D), dtype=jnp.float32)
        adj = jax.random.randint(ks[1], (2, E), 0, N, dtype=jnp.int64)
        edge_weights = jax.random.uniform(ks[2], (E,), dtype=jnp.float32)
        s = 1.0 / np.sqrt(D)
        W1 = jax.random.uniform(ks[3], (D, D), jnp.float32, -s, s)
        b1 = jnp.zeros((D,), jnp.float32)
        W2 = jax.random.uniform(ks[4], (D, D), jnp.float32, -s, s)
        b2 = jnp.zeros((D,), jnp.float32)
        return {'x': x, 'adj': adj, 'edge_weights': edge_weights, 'W1': W1, 'b1': b1, 'W2': W2, 'b2': b2}
    _L0_gnn_all = _L0_gnn_setup()
    _L0_gnn_in = {k: v for k, v in _L0_gnn_all.items() if k in ('W1', 'b1', 'W2', 'b2')}
    del _L0_gnn_all

    def _L1_gnn_setup():
        import jax, jax.numpy as jnp
        import numpy as np
        N_NODES = 6250
        N_EDGES = 100000
        H = 128
        LN_EPS = 1e-05
        key = jax.random.key(seed)
        ks = jax.random.split(key, 8)
        x = jax.random.normal(ks[0], (N_NODES, H), dtype=jnp.float32)
        edge_index = jax.random.randint(ks[1], (2, N_EDGES), 0, N_NODES, dtype=jnp.int64)
        W1 = jax.random.normal(ks[2], (2 * H, H), dtype=jnp.float32) * 0.02
        b1 = jnp.zeros((H,), dtype=jnp.float32)
        W2 = jax.random.normal(ks[3], (H, 1), dtype=jnp.float32) * 0.02
        b2 = jnp.zeros((1,), dtype=jnp.float32)
        gamma = jnp.ones((H,), dtype=jnp.float32)
        beta = jnp.zeros((H,), dtype=jnp.float32)
        return {'x': x, 'edge_index': edge_index, 'W1': W1, 'b1': b1, 'W2': W2, 'b2': b2, 'gamma': gamma, 'beta': beta}
    _L1_gnn_all = _L1_gnn_setup()
    _L1_gnn_in = {k: v for k, v in _L1_gnn_all.items() if k in ('W1', 'b1', 'W2', 'b2', 'gamma', 'beta')}
    del _L1_gnn_all
    return {'x': x, 'src': src, 'dst': dst, 'edge_weight': edge_weight, 'L0_gnn_W1': _L0_gnn_in['W1'], 'L0_gnn_b1': _L0_gnn_in['b1'], 'L0_gnn_W2': _L0_gnn_in['W2'], 'L0_gnn_b2': _L0_gnn_in['b2'], 'L1_gnn_W1': _L1_gnn_in['W1'], 'L1_gnn_b1': _L1_gnn_in['b1'], 'L1_gnn_W2': _L1_gnn_in['W2'], 'L1_gnn_b2': _L1_gnn_in['b2'], 'L1_gnn_gamma': _L1_gnn_in['gamma'], 'L1_gnn_beta': _L1_gnn_in['beta']}

def reference(x, src, dst, edge_weight, L0_gnn_W1, L0_gnn_b1, L0_gnn_W2, L0_gnn_b2, L1_gnn_W1, L1_gnn_b1, L1_gnn_W2, L1_gnn_b2, L1_gnn_gamma, L1_gnn_beta):
    import jax
    import jax.numpy as jnp

    def _L0_gnn_ref(x, adj, edge_weights, W1, b1, W2, b2):
        import jax, jax.numpy as jnp
        import numpy as np
        N, E, D = (6250, 75000, 128)

        def gcn_conv(x, edge_index, edge_weight, W, b, num_nodes):
            row, col = (edge_index[0], edge_index[1])
            deg = jax.ops.segment_sum(edge_weight, col, num_segments=num_nodes)
            dis = jnp.where(deg > 0, jax.lax.rsqrt(jnp.where(deg > 0, deg, 1.0)), 0.0)
            norm = dis[row] * edge_weight * dis[col]
            xl = x @ W
            msg = xl[row] * norm[:, None]
            out = jax.ops.segment_sum(msg, col, num_segments=num_nodes)
            return out + b
        res = x
        h = gcn_conv(x, adj, edge_weights, W1, b1, N)
        h = jax.nn.relu(h)
        h = gcn_conv(h, adj, edge_weights, W2, b2, N)
        h = jax.nn.relu(h)
        return h + res

    def _L1_gnn_ref(x, edge_index, W1, b1, W2, b2, gamma, beta):
        import jax, jax.numpy as jnp
        import numpy as np
        N_NODES = 6250
        N_EDGES = 100000
        H = 128
        LN_EPS = 1e-05
        src = edge_index[0]
        tgt = edge_index[1]
        edge_feat = jnp.concatenate([x[src], x[tgt]], axis=1)
        h = jax.nn.relu(edge_feat @ W1 + b1)
        w = jax.nn.sigmoid(h @ W2 + b2)[:, 0]
        agg = jax.ops.segment_sum(w[:, None] * x[src], tgt, num_segments=x.shape[0])
        attended = x + agg
        mu = jnp.mean(attended, axis=-1, keepdims=True)
        var = jnp.mean(jnp.square(attended - mu), axis=-1, keepdims=True)
        out = (attended - mu) * jax.lax.rsqrt(var + LN_EPS) * gamma + beta
        return out
    edge_index = jnp.stack([src, dst])
    h = jnp.maximum(_layernorm(x, axis=-1), 0.0)
    x = x + _L0_gnn_ref(h, edge_index, edge_weight, L0_gnn_W1, L0_gnn_b1, L0_gnn_W2, L0_gnn_b2)
    h = jnp.maximum(_layernorm(x, axis=-1), 0.0)
    x = x + _L1_gnn_ref(h, edge_index, L1_gnn_W1, L1_gnn_b1, L1_gnn_W2, L1_gnn_b2, L1_gnn_gamma, L1_gnn_beta)
    return x

_drawn_inputs = setup_inputs


def setup_inputs(seed=0):
    import zlib

    import numpy as np

    out = dict(_drawn_inputs(seed))
    spreads = {'L0_gnn_b1': (0.0, 0.1),
     'L0_gnn_b2': (0.0, 0.1),
     'L1_gnn_b1': (0.0, 0.8),
     'L1_gnn_gamma': (1.0, 0.2),
     'L1_gnn_beta': (0.0, 0.1)}
    factors = {'edge_weight': 8.0, 'L1_gnn_W1': 8.0, 'L1_gnn_W2': 8.0}
    for name, (base, spread) in spreads.items():
        noise = np.random.default_rng([zlib.crc32(name.encode()), seed]).standard_normal(out[name].shape)
        drawn = base * np.exp(spread * noise) if base else spread * noise
        out[name] = jnp.asarray(drawn.astype(out[name].dtype))
    for name, factor in factors.items():
        out[name] = (out[name] * factor).astype(out[name].dtype)
    return out
```

```python
import concourse.bass as bass
from concourse import mybir
from contextlib import ExitStack


P = 128
N, H, E = 6250, 128, 100000
WINDOWS = -(-N // P)
LAST = N - (WINDOWS - 1) * P
BLOCK = 16
RING = 8
TILES = -(-E // (P * BLOCK)) * BLOCK
CHUNKS = 7
ROWS = TILES // CHUNKS
EXTRAS = -(-(N // P) // BLOCK) * BLOCK
STEPS = TILES + EXTRAS
SUMS = (N // P + 2) * P
GROUP = 7
GROUPS = WINDOWS // GROUP
FULL = E // (P * ROWS)
TAIL = E // P - FULL * ROWS
REST = E - (E // P) * P
NOWHERE = 16384.0
EPS = 1e-5
TURN_LAG, GATE_LAG, SCORE_LAG, OPEN_LAG, SUM_LAG, ADD_LAG = 1, 2, 3, 3, 5, 8
RECORD = 4
SORT = 4
DIGIT = 7


def gnn_kernel(nc, x, src, dst, weight, g_w1, g_b1, g_w2, g_b2,
               a_w1, a_b1, a_w2, a_b2, gamma, beta, out, rows1, rows2, rows3, brows, records):
    f32, i32 = mybir.dt.float32, mybir.dt.int32
    ALU, ACT, AX = mybir.AluOpType, mybir.ActivationFunctionType, mybir.AxisListType
    ds = bass.ds

    ctx = ExitStack()
    with ctx:
        def sb(name, shape, dt=f32):
            return ctx.enter_context(nc.sbuf_tensor(name, shape, dt))

        def sem(name):
            return ctx.enter_context(nc.semaphore(name))

        bank = [ctx.enter_context(nc.psum_tensor(f"bank{i}", [P, 512], f32)) for i in range(8)]

        srcR = sb("srcR", [ROWS, CHUNKS, P], i32)
        dstR = sb("dstR", [ROWS, CHUNKS, P], i32)
        wR = sb("wR", [ROWS, CHUNKS, P])
        nextR = sb("nextR", [ROWS, CHUNKS, P], i32)
        srcF = sb("srcF", [ROWS, CHUNKS, P])
        dstF = sb("dstF", [ROWS, CHUNKS, P])
        localF = sb("localF", [ROWS, CHUNKS, P])
        cols = sb("cols", [ROWS, 9, CHUNKS])
        (VIOLATIONS,
         COUNT,
         TOTAL,
         THROUGH,
         UPTO,
         BEFORE,
         ORIGIN,
         SHIFT) = range(8)
        spanI = sb("spanI", [ROWS, 2, CHUNKS], i32)
        chosen = sb("chosen", [ROWS, CHUNKS, EXTRAS])
        srcT = sb("srcT", [P, STEPS], i32)
        localT = sb("localT", [P, STEPS])
        wT = sb("wT", [P, STEPS])
        baseT = sb("baseT", [1, STEPS], i32)
        dstT = sb("dstT", [P, TILES], i32)
        digitI = sb("digitI", [P, 2, TILES], i32)
        digits = sb("digits", [P, 2, TILES])
        flags = sb("flags", [1, 2], i32)

        iota = sb("iota", [P, P])
        ident = sb("ident", [P, P])
        upper = sb("upper", [P, P])
        ones = sb("ones", [P, P])
        zeros = sb("zeros", [P, P])
        W1 = sb("W1", [P, H])
        W2 = sb("W2", [P, H])
        AW = sb("AW", [P, 2, H])
        vec = sb("vec", [P, 6, H])
        ab2 = sb("ab2", [P, 1])

        X = sb("X", [P, WINDOWS, H])
        Hn = sb("Hn", [P, WINDOWS, H])
        T = sb("T", [P, WINDOWS, H])
        S = sb("S", [P, SUMS])
        stats = sb("stats", [P, WINDOWS, 6])
        mean = sb("mean", [P, WINDOWS])
        var = sb("var", [P, WINDOWS])
        rstd = sb("rstd", [P, WINDOWS])
        shift = sb("shift", [P, WINDOWS])
        deg = sb("deg", [P, 2, WINDOWS])
        spread = sb("spread", [P, WINDOWS])
        eps = sb("eps", [P, 1])
        dis = sb("dis", [P, WINDOWS])

        recF = T[:, 0:WINDOWS // 2 + 1, :].rearrange("p w f -> p (w f)")[:, 0:TILES * RECORD].rearrange(
            "p (t r) -> p t r", r=RECORD)
        recI = recF.bitcast(i32)
        strict = sb("strict", [P, P])
        moved = sb("moved", [P, SORT, RECORD], i32)
        place = sb("place", [P, SORT], i32)
        placeF = sb("placeF", [P, 1])
        counts = sb("counts", [P, 1])
        start = sb("start", [1, P])
        reached = sb("reached", [1, P])

        picked = sb("picked", [P, 2, RING], i32)
        msg = sb("msg", [P, BLOCK, 2 * H])
        hot = sb("hot", [P, BLOCK, P])
        hotT = sb("hotT", [P, 4, P])
        gated = sb("gated", [P, 4, P])
        bwin = sb("bwin", [P, BLOCK, H])
        junk = sb("junk", [P, 2, P])
        score = sb("score", [P, RING])
        gate = sb("gate", [P, RING])

        s_const = sem("s_const")
        s_in = sem("s_in")
        s_pad = sem("s_pad")
        s_weights = sem("s_weights")
        s_x = sem("s_x")
        s_xpad = sem("s_xpad")
        s_dve = sem("s_dve")
        s_pre = sem("s_pre")
        s_prep = sem("s_prep")
        s_flag = sem("s_flag")
        s_sclear = sem("s_sclear")
        s_sload = sem("s_sload")
        s_skeys = sem("s_skeys")
        s_shot = sem("s_shot")
        s_scount = sem("s_scount")
        s_stotal = sem("s_stotal")
        s_scounts = sem("s_scounts")
        s_sstart = sem("s_sstart")
        s_sstarted = sem("s_sstarted")
        s_smark = sem("s_smark")
        s_srank = sem("s_srank")
        s_splace = sem("s_splace")
        s_swrite = [sem(f"s_swrite{j}") for j in range(SORT)]
        s_sfree = sem("s_sfree")
        s_srows = sem("s_srows")
        s_steps = sem("s_steps")
        s_low = sem("s_low")
        s_high = sem("s_high")
        s_deg = sem("s_deg")
        s_total = sem("s_total")
        s_var = sem("s_var")
        s_root = sem("s_root")
        s_scale = sem("s_scale")
        s_stat = sem("s_stat")
        s_h = sem("s_h")
        s_scaled = sem("s_scaled")
        s_zeroed = sem("s_zeroed")
        s_product = sem("s_product")
        s_applied = sem("s_applied")
        s_rows = sem("s_rows")
        s_table = sem("s_table")
        s_added = sem("s_added")
        s_flip = sem("s_flip")
        s_flipped = sem("s_flipped")
        s_ab = sem("s_ab")
        s_abread = sem("s_abread")
        s_tables = sem("s_tables")
        s_back = sem("s_back")
        s_attended = sem("s_attended")
        s_normed = sem("s_normed")
        s_final = sem("s_final")
        s_issue = sem("s_issue")
        s_out = sem("s_out")

        class Lane:
            def __init__(self, tag):
                self.listed = [sem(f"listed{i}{tag}") for i in range(2)]
                self.gathered = [sem(f"gathered{i}{tag}") for i in range(BLOCK)]
                self.loaded = [sem(f"loaded{i}{tag}") for i in range(BLOCK)]
                self.hot = sem(f"hot{tag}")
                self.done = sem(f"done{tag}")
                self.added = sem(f"added{tag}")
                self.turned = sem(f"turned{tag}")
                self.hotT = sem(f"hotT{tag}")
                self.z = sem(f"z{tag}")
                self.scored = sem(f"scored{tag}")
                self.opened = sem(f"opened{tag}")
                self.gated = sem(f"gated{tag}")

        main, extra = Lane(""), Lane("x")
        LANES = ((main, 0, TILES), (extra, TILES, EXTRAS))
        DONE0, ADDED0, DEG0, HOTT0, SCORED0 = 16, 8, RING, 2, 2

        def sweep(engine, blocks, stages):
            def place(i, j):
                for lag, do in stages:
                    before = (lag - j + BLOCK - 1) // BLOCK if lag > j else 0
                    if not isinstance(i, int) or 0 <= i - before < blocks:
                        do(i - before if before else i, j - lag + before * BLOCK)

            for j in range(BLOCK):
                place(0, j)
            with engine.Fori(1, blocks) as i:
                for j in range(BLOCK):
                    place(i, j)
            for j in range(max(lag for lag, _ in stages)):
                place(blocks, j)

        def flip_bank(w):
            return w % GROUP % 3

        def ab_bank(w):
            return 3 + w % GROUP % 4

        block = ctx.enter_context(nc.Block())

        @block.sync
        def _(sp):
            def rows_of(a, first, rest):
                whole = first + FULL * ROWS * P
                tail = whole + TAIL * P
                return (a[first:whole].rearrange("(k q j) -> q k j", q=ROWS, j=P),
                        a[whole:tail].rearrange("(q j) -> q j", j=P),
                        a[tail:tail + rest].rearrange("(q j) -> q j", q=1))

            sp.wait_ge(s_pad, 1)
            for dest, a, first, rest in ((dstR, dst, 0, REST), (nextR, dst, 1, REST - 1),
                                         (srcR, src, 0, REST), (wR, weight, 0, REST)):
                whole, tail, last = rows_of(a, first, rest)
                sp.dma_start(dest[:, 0:FULL, :], whole).then_inc(s_in, 16)
                sp.dma_start(dest[0:TAIL, FULL, :], tail).then_inc(s_in, 16)
                sp.dma_start(dest[TAIL:TAIL + 1, FULL, 0:rest], last).then_inc(s_in, 16)
            sp.dma_start(X[:, 0:WINDOWS - 1, :],
                         x[0:(WINDOWS - 1) * P, :].rearrange("(w p) f -> p w f", p=P)).then_inc(s_x, 16)
            sp.wait_ge(s_xpad, 1)
            sp.dma_start(X[0:LAST, WINDOWS - 1, :], x[(WINDOWS - 1) * P:N, :]).then_inc(s_x, 16)
            sp.dma_start(W1[:, :], g_w1).then_inc(s_weights, 16)
            sp.dma_start(W2[:, :], g_w2).then_inc(s_weights, 16)
            sp.dma_start(AW[:, :, :], a_w1.rearrange("(k p) f -> p k f", p=P)).then_inc(s_weights, 16)
            for n, v in enumerate((g_b1, g_b2, a_b1, a_w2.rearrange("f o -> (f o)"), gamma, beta)):
                sp.dma_start(vec[:, n, :], v.unsqueeze(0).to_broadcast([P, H])).then_inc(s_weights, 16)
            sp.dma_start(ab2[:, :], a_b2.unsqueeze(0).to_broadcast([P, 1])).then_inc(s_weights, 16)

            def nodes(table, g, cols=slice(0, H)):
                return table[g * GROUP * P:(g + 1) * GROUP * P, cols].rearrange("(w p) f -> p w f", p=P)

            def group(a, g):
                return a[:, g * GROUP:(g + 1) * GROUP, :]

            sp.wait_ge(s_flag, 1)
            disorder = sp.value_load(flags[0:1, 0:1])
            with sp.If(disorder > 0), nc.allow_non_contiguous_dma(reason="edges out of order only"):
                sp.wait_ge(s_sclear, 1)
                whole = E // P * P
                for n, (a, rec) in enumerate(((src, recI), (dst, recI), (weight, recF))):
                    sp.dma_start(rec[:, 0:E // P, n], a[0:whole].rearrange("(t p) -> p t", p=P)
                                 ).then_inc(s_sload, 16)
                    sp.dma_start(rec[0:REST, E // P, n:n + 1], a[whole:E].rearrange("(p t) -> p t", t=1)
                                 ).then_inc(s_sload, 16)
                for j in range(SORT):
                    sp.wait_ge(s_swrite[j], 16 * (TILES // SORT))
                sp.dma_start(recI[:, :, :], records.rearrange("(t p) r -> p t r", p=P)).then_inc(s_sload, 16)
                for j in range(SORT):
                    sp.wait_ge(s_swrite[j], 2 * 16 * (TILES // SORT))
                for n, rows in enumerate((srcR, dstR, wR[:, :, :].bitcast(i32))):
                    for k in range(CHUNKS):
                        sp.dma_start(rows[:, k, :], records[k * ROWS * P:(k + 1) * ROWS * P, n].rearrange(
                            "(q j) -> q j", j=P)).then_inc(s_srows, 16)
            sp.wait_ge(s_steps, 1)
            extras = sp.value_load(flags[0:1, 1:2])

            def edges(layer, lane_no):
                lane, first, count = LANES[lane_no]
                blocks = count // BLOCK

                def indices(i, j):
                    if j % RING:
                        return
                    half = j // RING
                    if not (isinstance(i, int) and i + layer == 0):
                        for slot in range(half * RING, (half + 1) * RING):
                            sp.wait_ge(lane.gathered[slot], i * 16 + 16 * layer * blocks)
                    sp.dma_start(picked[:, half, :], srcT[:, ds(i * BLOCK + (first + j), RING)]
                                 ).then_inc(lane.listed[half], 16)

                def rows(i, j):
                    base = sp.value_load(baseT[0:1, ds(i * BLOCK + (first + j), 1)],
                                         min_val=0, max_val=SUMS - P)
                    sp.wait_ge(lane.done, i * BLOCK + (layer * count + j + DONE0 - BLOCK + 1))
                    sp.dma_start(bwin[:, j, :], brows[ds(base, P), :]).then_inc(lane.loaded[j], 16)

                sweep(sp, blocks, [(0, indices)] + [(0, rows)] * (layer == 2))

            for layer in range(3):
                if layer == 0:
                    for g in range(GROUPS):
                        sp.wait_ge(s_scaled, g + 1)
                        sp.dma_start(nodes(rows1, g), group(T, g)).then_inc(s_table, 16)
                elif layer == 1:
                    for g in range(GROUPS):
                        sp.wait_ge(s_rows, (g + 1) * GROUP)
                        sp.dma_start(nodes(rows2, g), group(T, g)).then_inc(s_table, 16)
                else:
                    for g in range(GROUPS):
                        sp.wait_ge(s_abread, (g + 1) * GROUP)
                        sp.dma_start(nodes(rows3, g), group(Hn, g)).then_inc(s_tables, 16)
                        sp.dma_start(nodes(rows3, g, slice(H, 2 * H)), group(T, g)).then_inc(s_tables, 16)
                        sp.dma_start(nodes(brows, g), S[:, g * GROUP * P:(g + 1) * GROUP * P].rearrange(
                            "p (w f) -> p w f", f=H)).then_inc(s_tables, 16)
                    sp.dma_start(brows[WINDOWS * P:SUMS, :], zeros[:, :]).then_inc(s_tables, 16)
                    sp.wait_ge(s_tables, 16 * (3 * GROUPS + 1))
                edges(layer, 0)
                with sp.If(extras > 0):
                    sp.wait_ge(main.done, DONE0 + (layer + 1) * TILES)
                    edges(layer, 1)

            for g in range(GROUPS):
                sp.wait_ge(s_final, g + 1)
                full = GROUP if g < GROUPS - 1 else GROUP - 1
                w0 = g * GROUP
                sp.dma_start(out[w0 * P:(w0 + full) * P, :].rearrange("(w p) f -> p w f", p=P),
                             T[:, w0:w0 + full, :]).then_inc(s_out, 16)
            sp.dma_start(out[(WINDOWS - 1) * P:N, :], T[0:LAST, WINDOWS - 1, :]).then_inc(s_out, 16)
            sp.wait_ge(s_out, 16 * (GROUPS + 1))

        @block.gpsimd
        def _(pool):
            pool.memset(ones[:, :], 1.0).then_inc(s_const, 1)
            pool.memset(zeros[:, :], 0.0).then_inc(s_const, 1)
            pool.iota(iota[:, :], [[1, P]], base=0, channel_multiplier=0,
                      allow_small_or_imprecise_dtypes=True).then_inc(s_const, 1)
            pool.wait_ge(s_const, 3)
            pool.affine_select(out=ident[:, :], in_=ones[:, :], pattern=[[1, P]], compare_op=ALU.is_equal,
                               fill=0.0, base=0, channel_multiplier=-1).then_inc(s_const, 1)
            pool.affine_select(out=strict[:, :], in_=ones[:, :], pattern=[[1, P]], compare_op=ALU.is_gt,
                               fill=0.0, base=0, channel_multiplier=-1).then_inc(s_const, 1)
            pool.affine_select(out=upper[:, :], in_=ones[:, :], pattern=[[1, P]], compare_op=ALU.is_ge,
                               fill=0.0, base=0, channel_multiplier=-1).then_inc(s_const, 1)
            pool.wait_ge(s_flag, 1)
            disorder = pool.value_load(flags[0:1, 0:1])
            with pool.If(disorder > 0):
                for digit in range(2):
                    if digit == 1:
                        pool.wait_ge(s_sload, 16 * 7)
                    with pool.Fori(0, TILES // SORT) as i:
                        for j in range(SORT):
                            pool.wait_ge(s_splace, i * SORT + (digit * TILES + j + 1))
                            pool.sem_inc(s_issue, 1)
                            pool.indirect_dma_start(
                                out=records[:, :], out_offset=bass.IndirectOffsetOnAxis(ap=place[:, j:j + 1], axis=0),
                                in_=moved[:, j, :], in_offset=None).then_inc(s_swrite[j], 16)
                        for j in range(SORT):
                            pool.wait_ge(s_swrite[j], i * 16 + 16 * (digit * (TILES // SORT) + 1))
                        pool.sem_inc(s_sfree, SORT)
            pool.wait_ge(s_steps, 1)
            extras = pool.value_load(flags[0:1, 1:2])

            def gathers(layer, lane_no):
                lane, first, count = LANES[lane_no]
                table, width = ((rows1, H), (rows2, H), (rows3, 2 * H))[layer]
                def gather(i, j):
                    half = j // RING
                    if j % RING == 0:
                        pool.wait_ge(lane.listed[half], i * 16 + 16 * (layer * (count // BLOCK) + 1))
                    if j % 4 == 0:
                        pool.wait_ge(lane.done, i * BLOCK + (layer * count + j + 3 + DONE0 - BLOCK + 1))
                        pool.sem_inc(s_issue, 1)
                    pool.indirect_dma_start(
                        out=msg[:, j, 0:width], out_offset=None, in_=table[:, :],
                        in_offset=bass.IndirectOffsetOnAxis(ap=picked[:, half, j % RING:j % RING + 1], axis=0),
                    ).then_inc(lane.gathered[j], 16)

                with pool.Fori(0, count // BLOCK) as i:
                    for j in range(BLOCK):
                        gather(i, j)

            for layer in range(3):
                if layer < 2:
                    pool.wait_ge(s_table, 16 * GROUPS * (layer + 1))
                else:
                    pool.wait_ge(s_tables, 16 * (3 * GROUPS + 1))
                gathers(layer, 0)
                with pool.If(extras > 0):
                    pool.wait_ge(main.done, DONE0 + (layer + 1) * TILES)
                    gathers(layer, 1)

        @block.tensor
        def _(pe):
            pe.sem_inc(main.done, DONE0)
            pe.sem_inc(extra.done, DONE0)
            pe.sem_inc(s_deg, DEG0)
            pe.wait_ge(s_const, 6)
            pe.wait_ge(s_pre, 1)
            pe.matmul(bank[0][:, 0:1], ones[0:ROWS, :], cols[0:ROWS, VIOLATIONS, 0:1],
                      start=True, stop=True).then_inc(s_prep, 1)

            pe.wait_ge(s_flag, 1)
            disorder = pe.value_load(flags[0:1, 0:1])
            with pe.If(disorder > 0):
                pe.sem_inc(s_scount, SORT)
                for digit in range(2):
                    pe.matmul(bank[0][:, 0:1], zeros[:, :], zeros[:, 0:1], start=True, stop=False,
                              skip_group_check=True)
                    with pe.Fori(0, TILES // SORT) as i:
                        for j in range(SORT):
                            pe.wait_ge(s_shot, i * SORT + (digit * TILES + j + 1))
                            pe.matmul(bank[0][:, 0:1], hot[:, j, :], ones[:, 0:1], start=False, stop=False,
                                      skip_group_check=True).then_inc(s_scount, 1)
                    pe.matmul(bank[0][:, 0:1], zeros[:, :], zeros[:, 0:1], start=False, stop=True,
                              skip_group_check=True).then_inc(s_stotal, 1)
                    pe.wait_ge(s_scounts, digit + 1)
                    pe.matmul(bank[1][0:1, 0:P], counts[:, :], strict[:, :], start=True, stop=True
                              ).then_inc(s_sstart, 1)
                    pe.wait_ge(s_sstarted, digit + 1)
                    pe.matmul(bank[3][0:1, 0:P], ones[0:1, 0:1], start[:, :], start=True, stop=False,
                              skip_group_check=True)
                    with pe.Fori(0, TILES // SORT) as i:
                        for j in range(SORT):
                            pe.wait_ge(s_smark, i * SORT + (digit * TILES + j + 1))
                            pe.matmul(bank[2][:, 0:P], strict[:, :], hot[:, 8 + j, :], start=True, stop=False)
                            pe.matmul(bank[2][:, 0:P], ones[0:1, :], reached[:, :], start=False, stop=True)
                            pe.matmul(bank[3][0:1, 0:P], ones[:, 0:1], hot[:, 8 + j, :], start=False, stop=False,
                                      skip_group_check=True).then_inc(s_srank, 1)
                    pe.wait_ge(s_splace, (digit + 1) * TILES)
                    pe.matmul(bank[3][0:1, 0:P], zeros[:, 0:1], zeros[:, :], start=False, stop=True,
                              skip_group_check=True)

            pe.wait_ge(s_pre, 2)
            pe.matmul(bank[1][0:ROWS, 0:CHUNKS], upper[0:ROWS, 0:ROWS], cols[0:ROWS, COUNT, :],
                      start=True, stop=True).then_inc(s_prep, 1)
            pe.matmul(bank[2][:, 0:CHUNKS], ones[0:ROWS, :], cols[0:ROWS, COUNT, :],
                      start=True, stop=True).then_inc(s_prep, 1)
            pe.wait_ge(s_pre, 3)
            for a, rows in enumerate((srcF, localF, wR, dstF)):
                for k in range(CHUNKS):
                    last = pe.transpose(bank[2 * a + k // 4][:, (k % 4) * ROWS:(k % 4 + 1) * ROWS],
                                        rows[:, k, :], ident[0:ROWS, 0:ROWS])
                last.then_inc(s_prep, 1)
            pe.wait_ge(s_pre, 4)
            for a, rows in enumerate((srcF, localF, wR)):
                for k in range(CHUNKS):
                    last = pe.matmul(bank[a][:, 0:EXTRAS], rows[:, k, :], chosen[:, k, :],
                                     start=(k == 0), stop=(k == CHUNKS - 1))
                last.then_inc(s_prep, 1)
            for k in range(CHUNKS):
                last = pe.matmul(bank[3][0:1, 0:EXTRAS], cols[0:ROWS, ORIGIN, k:k + 1], chosen[:, k, :],
                                 start=(k == 0), stop=(k == CHUNKS - 1))
            last.then_inc(s_prep, 1)

            pe.matmul(bank[7][:, 0:WINDOWS], zeros[:, :], zeros[:, 0:WINDOWS], start=True, stop=False,
                      skip_group_check=True)
            with pe.Fori(0, TILES // BLOCK) as i:
                for j in range(BLOCK):
                    pe.wait_ge(s_low, i * BLOCK + (j + 1))
                    pe.wait_ge(s_high, i * BLOCK + (j + 1))
                    pe.matmul(bank[7][:, 0:WINDOWS], msg[:, j % RING, 0:P], hot[:, j % RING, 0:WINDOWS],
                              start=False, stop=False, skip_group_check=True).then_inc(s_deg, 1)
            pe.matmul(bank[7][:, 0:WINDOWS], zeros[:, :], zeros[:, 0:WINDOWS], start=False, stop=True,
                      skip_group_check=True).then_inc(s_total, 1)
            extras = pe.value_load(flags[0:1, 1:2])

            def products(layer, lane_no):
                lane, first, count = LANES[lane_no]
                blocks = count // BLOCK

                def rows_here(i, j):
                    pe.wait_ge(lane.gathered[j], i * 16 + 16 * (layer * blocks + 1))

                def bank_free(i, j):
                    pe.wait_ge(lane.added, i * BLOCK + (layer * count + j + ADDED0 - 4 + 1))

                def summed(i, j):
                    rows_here(i, j)
                    pe.wait_ge(lane.hot, i * BLOCK + (layer * count + j + 1))
                    bank_free(i, j)
                    pe.matmul(bank[j % 4][:, 0:P], msg[:, j, 0:H], hot[:, j, :],
                              start=True, stop=True).then_inc(lane.done, 1)

                def turn(i, j):
                    pe.wait_ge(lane.hot, i * BLOCK + (layer * count + j + 1))
                    pe.wait_ge(lane.hotT, i * BLOCK + (j + HOTT0 - 2 + 1))
                    pe.transpose(bank[4 + j % 2][:, 0:P], hot[:, j, :],
                                 ident[:, :]).then_inc(lane.turned, 1)

                def gate_input(i, j):
                    rows_here(i, j)
                    pe.wait_ge(lane.loaded[j], i * 16 + 16)
                    pe.wait_ge(lane.hotT, i * BLOCK + (j + HOTT0 + 1))
                    pe.wait_ge(lane.scored, i * BLOCK + (j + SCORED0 - 2 + 1))
                    pe.matmul(bank[6 + j % 2][:, 0:H], hotT[:, j % 4, :], bwin[:, j, :],
                              start=True, stop=False)
                    pe.matmul(bank[6 + j % 2][:, 0:H], ident[:, :], msg[:, j, H:2 * H],
                              start=False, stop=True).then_inc(lane.z, 1)

                def gated_sum(i, j):
                    pe.wait_ge(lane.gated, i * BLOCK + (j + 1))
                    bank_free(i, j)
                    pe.matmul(bank[j % 4][:, 0:P], msg[:, j, 0:H], gated[:, j % 4, :],
                              start=True, stop=True).then_inc(lane.done, 1)

                if layer < 2:
                    sweep(pe, blocks, [(0, summed)])
                else:
                    sweep(pe, blocks, [(TURN_LAG, turn), (GATE_LAG, gate_input), (SUM_LAG, gated_sum)])

            def earlier(w, slot):
                same = [v for v in range(w) if slot(v) == slot(w)]
                return same[-1] if same else None

            for layer in range(3):
                if layer == 2:
                    pe.wait_ge(s_abread, WINDOWS)
                products(layer, 0)
                with pe.If(extras > 0):
                    pe.wait_ge(main.added, ADDED0 + (layer + 1) * TILES)
                    products(layer, 1)
                if layer < 2:
                    pe.wait_ge(s_weights, 16 * 10)
                    pe.wait_ge(main.added, ADDED0 + (layer + 1) * TILES)
                    with pe.If(extras > 0):
                        pe.wait_ge(extra.added, ADDED0 + (layer + 1) * EXTRAS)
                    for w in range(WINDOWS):
                        n = layer * WINDOWS + w
                        if n >= GROUP:
                            pe.wait_ge(s_applied, n - GROUP + 1)
                        pe.matmul(bank[w % GROUP][:, 0:H], S[:, w * P:(w + 1) * P], (W1, W2)[layer][:, :],
                                  start=True, stop=True).then_inc(s_product, 1)
                if layer == 1:
                    pe.wait_ge(s_applied, 2 * WINDOWS)
                    for w in range(WINDOWS + 1):
                        if w < WINDOWS:
                            pe.wait_ge(s_h, WINDOWS + w + 1)
                            v = earlier(w, flip_bank)
                            if v is not None:
                                pe.wait_ge(s_flipped, v + 1)
                            pe.transpose(bank[flip_bank(w)][:, 0:P], Hn[:, w, :],
                                         ident[:, :]).then_inc(s_flip, 1)
                        if w >= 1:
                            u = w - 1
                            pe.wait_ge(s_flipped, u + 1)
                            v = earlier(u, ab_bank)
                            if v is not None:
                                pe.wait_ge(s_abread, v + 1)
                            pe.matmul(bank[ab_bank(u)][:, 0:2 * H], hot[:, u % GROUP, :],
                                      AW[:, :, :].rearrange("p k f -> p (k f)"),
                                      start=True, stop=True).then_inc(s_ab, 1)
                if layer == 2:
                    pe.wait_ge(main.added, ADDED0 + 3 * TILES)
                    with pe.If(extras > 0):
                        pe.wait_ge(extra.added, ADDED0 + 3 * EXTRAS)
                    for w in range(WINDOWS):
                        if w >= GROUP:
                            pe.wait_ge(s_attended, w - GROUP + 1)
                        pe.transpose(bank[w % GROUP][:, 0:P], S[:, w * P:(w + 1) * P],
                                     ident[:, :]).then_inc(s_back, 1)

        @block.scalar
        def _(act):
            for lane in (main, extra):
                act.sem_inc(lane.hotT, HOTT0)
            act.wait_ge(s_var, 1)
            act.activation(spread[:, :], var[:, :], ACT.Sqrt, bias=eps[:, 0:1]).then_inc(s_root, 1)
            act.wait_ge(s_scale, 1)
            with act.Fori(0, WINDOWS) as w:
                act.activation(Hn[:, ds(w, 1), :], X[:, ds(w, 1), :], ACT.Relu, bias=shift[:, ds(w, 1)],
                               scale=rstd[:, ds(w, 1)]).then_inc(s_h, 1)
            act.wait_ge(s_var, 2)
            act.activation(spread[:, :], deg[:, 1, :], ACT.Sqrt).then_inc(s_root, 1)
            act.wait_ge(s_steps, 1)
            extras = act.value_load(flags[0:1, 1:2])

            with act.Fori(0, WINDOWS) as w:
                act.wait_ge(s_applied, w + 1)
                act.activation(T[:, ds(w, 1), :], T[:, ds(w, 1), :], ACT.Relu,
                               scale=dis[:, ds(w, 1)]).then_inc(s_rows, 1)

            act.wait_ge(s_var, 3)
            act.activation(spread[:, :], var[:, :], ACT.Sqrt, bias=eps[:, 0:1]).then_inc(s_root, 1)
            act.wait_ge(s_scale, 2)
            with act.Fori(0, WINDOWS) as w:
                act.activation(Hn[:, ds(w, 1), :], X[:, ds(w, 1), :], ACT.Relu, bias=shift[:, ds(w, 1)],
                               scale=rstd[:, ds(w, 1)]).then_inc(s_h, 1)
            with act.Fori(0, GROUPS) as g:
                for k in range(GROUP):
                    act.wait_ge(s_flip, g * GROUP + (k + 1))
                    act.activation(hot[:, k, :], bank[flip_bank(k)][:, 0:P], ACT.Copy).then_inc(s_flipped, 1)

            def gates(lane_no):
                lane, first, count = LANES[lane_no]

                def copy(i, j):
                    act.wait_ge(lane.turned, i * BLOCK + (j + 1))
                    act.activation(hotT[:, j % 4, :], bank[4 + j % 2][:, 0:P], ACT.Copy).then_inc(lane.hotT, 1)

                def opened(i, j):
                    act.wait_ge(lane.scored, i * BLOCK + (j + SCORED0 + 1))
                    act.activation(gate[:, j % RING:j % RING + 1], score[:, j % RING:j % RING + 1],
                                   ACT.Sigmoid, bias=ab2[:, 0:1]).then_inc(lane.opened, 1)

                def times(i, j):
                    act.wait_ge(lane.opened, i * BLOCK + (j + 1))
                    act.wait_ge(lane.done, i * BLOCK + (2 * count + j + DONE0 - 4 + 1))
                    act.activation(gated[:, j % 4, :], hot[:, j, :], ACT.Copy,
                                   scale=gate[:, j % RING:j % RING + 1]).then_inc(lane.gated, 1)

                sweep(act, count // BLOCK, [(TURN_LAG, copy), (OPEN_LAG, opened), (OPEN_LAG + 1, times)])

            gates(0)
            with act.If(extras > 0):
                gates(1)

            act.wait_ge(s_var, 4)
            act.activation(spread[:, :], var[:, :], ACT.Sqrt, bias=eps[:, 0:1]).then_inc(s_root, 1)
            act.wait_ge(s_scale, 3)
            with act.Fori(0, WINDOWS) as w:
                act.activation(T[:, ds(w, 1), :], Hn[:, ds(w, 1), :], ACT.Identity, bias=shift[:, ds(w, 1)],
                               scale=rstd[:, ds(w, 1)]).then_inc(s_normed, 1)

        @block.vector
        def _(dve):
            chained = [0]

            def link(ins):
                chained[0] += 1
                ins.then_inc(s_dve, 1)
                dve.wait_ge(s_dve, chained[0])

            for lane in (main, extra):
                dve.sem_inc(lane.added, ADDED0)
                dve.sem_inc(lane.scored, SCORED0)
            dve.memset(dstR[:, FULL, :], N)
            dve.memset(nextR[:, FULL, :], N)
            dve.memset(srcR[:, FULL, :], 0)
            link(dve.memset(wR[:, FULL, :], 0.0))
            dve.drain().then_inc(s_pad, 1)
            dve.memset(eps[:, :], EPS)
            dve.memset(X[:, WINDOWS - 1, :], 0.0).then_inc(s_xpad, 1)

            def col(n):
                return cols[0:ROWS, n, :]

            dve.wait_ge(s_in, 16 * 12)
            dve.wait_ge(s_const, 6)
            link(dve.tensor_tensor(srcF[:, :, :], nextR[:, :, :], dstR[:, :, :], ALU.is_lt))
            link(dve.tensor_reduce(col(VIOLATIONS), srcF[:, :, :], AX.X, ALU.add))
            link(dve.tensor_reduce(cols[0:ROWS, VIOLATIONS, 0:1], col(VIOLATIONS), AX.X, ALU.add))
            dve.drain().then_inc(s_pre, 1)
            dve.wait_ge(s_prep, 1)
            link(dve.tensor_copy(flags[0:1, 0:1], bank[0][0:1, 0:1]))
            dve.drain().then_inc(s_flag, 1)
            disorder = dve.value_load(flags[0:1, 0:1])
            with dve.If(disorder > 0):
                dve.sem_inc(s_sfree, SORT)
                dve.memset(recI[:, :, :], 0)
                dve.drain()
                dve.memset(recI[:, E // P:TILES, 1], N)
                dve.drain().then_inc(s_sclear, 1)
                for digit in range(2):
                    dve.wait_ge(s_sload, 16 * (6 + digit))
                    dve.tensor_scalar(digitI[:, 0, :], recI[:, :, 1], (P - 1, DIGIT)[digit], None,
                                      (ALU.bitwise_and, ALU.logical_shift_right)[digit])
                    dve.drain()
                    dve.tensor_copy(digits[:, 0, :], digitI[:, 0, :])
                    dve.drain()
                    with dve.Fori(0, TILES // SORT) as i:
                        for j in range(SORT):
                            dve.wait_ge(s_scount, i * SORT + (digit * TILES + j + 1))
                            dve.tensor_scalar(hot[:, j, :], iota[:, :], digits[:, 0, ds(i * SORT + j, 1)],
                                              None, ALU.is_equal).then_inc(s_shot, 1)
                    dve.wait_ge(s_stotal, digit + 1)
                    dve.tensor_copy(counts[:, :], bank[0][:, 0:1]).then_inc(s_scounts, 1)
                    dve.wait_ge(s_sstart, digit + 1)
                    dve.tensor_copy(start[:, :], bank[1][0:1, 0:P])
                    dve.tensor_copy(reached[:, :], bank[1][0:1, 0:P])
                    dve.drain().then_inc(s_sstarted, 1)
                    with dve.Fori(0, TILES // SORT) as i:
                        for j in range(SORT):
                            t = i * SORT + j
                            dve.tensor_scalar(hot[:, 8 + j, :], iota[:, :], digits[:, 0, ds(t, 1)],
                                              None, ALU.is_equal).then_inc(s_smark, 1)
                            if j == 0:
                                dve.wait_ge(s_sfree, i * SORT + (digit * TILES + SORT))
                            dve.tensor_copy(moved[:, j, :], recI[:, ds(t, 1), :].rearrange("p t r -> p (t r)"))
                            dve.wait_ge(s_srank, i * SORT + (digit * TILES + j + 1))
                            dve.scalar_tensor_tensor(junk[:, 0, :], bank[2][:, 0:P], 1.0, hot[:, 8 + j, :],
                                                     ALU.mult, ALU.mult, accum_out=placeF[:, 0:1])
                            dve.tensor_copy(reached[:, :], bank[3][0:1, 0:P])
                            dve.drain()
                            dve.tensor_copy(place[:, j:j + 1], placeF[:, :]).then_inc(s_splace, 1)
                dve.wait_ge(s_srows, 16 * 3 * CHUNKS)
            dve.tensor_copy(srcF[:, :, :], srcR[:, :, :])
            link(dve.tensor_copy(dstF[:, :, :], dstR[:, :, :]))
            for k in range(CHUNKS):
                dve.tensor_scalar(localF[:, k, :], dstF[:, k, :], dstF[:, k, 0:1], None, ALU.subtract)
            link(dve.tensor_tensor(spanI[:, 0, :], dstR[:, :, P - 1], dstR[:, :, 0], ALU.subtract))
            link(dve.tensor_scalar(spanI[:, 1, :], spanI[:, 0, :], DIGIT, None, ALU.arith_shift_right))
            link(dve.tensor_copy(col(COUNT), spanI[:, 1, :]))
            dve.drain().then_inc(s_pre, 1)
            dve.wait_ge(s_prep, 3)
            link(dve.tensor_copy(col(TOTAL), bank[2][0:ROWS, 0:CHUNKS]))
            link(dve.tensor_tensor_scan(col(THROUGH), ones[0:ROWS, 0:CHUNKS], col(TOTAL), 0.0, ALU.mult, ALU.add))
            link(dve.tensor_copy(flags[0:1, 1:2], cols[0:1, THROUGH, CHUNKS - 1:CHUNKS]))
            link(dve.tensor_tensor(col(THROUGH), col(THROUGH), col(TOTAL), ALU.subtract))
            link(dve.tensor_tensor(col(UPTO), bank[1][0:ROWS, 0:CHUNKS], col(THROUGH), ALU.add))
            dve.drain().then_inc(s_pre, 1)
            link(dve.tensor_tensor(col(BEFORE), col(UPTO), col(COUNT), ALU.subtract))
            link(dve.tensor_scalar(col(ORIGIN), col(BEFORE), -float(P), float(P), ALU.mult, ALU.add))
            dve.tensor_scalar(col(SHIFT), col(ORIGIN), -1.0, NOWHERE, ALU.mult, ALU.add)
            link(dve.tensor_tensor(col(ORIGIN), col(ORIGIN), dstF[:, :, 0], ALU.add))

            banks4 = 4 * ROWS
            for a, dest in enumerate((srcT, localT, wT, dstT)):
                dve.wait_ge(s_prep, 4 + a)
                dve.tensor_copy(dest[:, 0:banks4], bank[2 * a][:, 0:banks4])
                dve.tensor_copy(dest[:, banks4:TILES], bank[2 * a + 1][:, 0:TILES - banks4])
                if a == 3:
                    dve.tensor_copy(baseT[0:1, 0:banks4], bank[2 * a][0:1, 0:banks4])
                    link(dve.tensor_copy(baseT[0:1, banks4:TILES], bank[2 * a + 1][0:1, 0:TILES - banks4]))

            for k in range(CHUNKS):
                link(dve.tensor_scalar(chosen[:, k, :], iota[0:ROWS, 0:EXTRAS], cols[0:ROWS, UPTO, k:k + 1],
                                       None, ALU.is_lt))
                link(dve.scalar_tensor_tensor(chosen[:, k, :], iota[0:ROWS, 0:EXTRAS],
                                              cols[0:ROWS, BEFORE, k:k + 1], chosen[:, k, :],
                                              ALU.is_ge, ALU.mult))
                link(dve.tensor_scalar(localF[:, k, :], localF[:, k, :], cols[0:ROWS, SHIFT, k:k + 1],
                                       None, ALU.add))
            dve.drain().then_inc(s_pre, 1)
            link(dve.tensor_scalar(digitI[:, 0, :], dstT[:, :], P - 1, None, ALU.bitwise_and))
            link(dve.tensor_scalar(digitI[:, 1, :], dstT[:, :], DIGIT, None, ALU.logical_shift_right))
            link(dve.tensor_copy(digits[:, :, :], digitI[:, :, :]))
            dve.wait_ge(s_prep, 11)
            dve.tensor_copy(srcT[:, TILES:STEPS], bank[0][:, 0:EXTRAS])
            dve.scalar_tensor_tensor(localT[:, TILES:STEPS], iota[:, 0:EXTRAS], -float(P),
                                     bank[1][:, 0:EXTRAS], ALU.mult, ALU.add)
            dve.tensor_copy(wT[:, TILES:STEPS], bank[2][:, 0:EXTRAS])
            dve.scalar_tensor_tensor(baseT[0:1, TILES:STEPS], iota[0:1, 0:EXTRAS], float(P),
                                     bank[3][0:1, 0:EXTRAS], ALU.mult, ALU.add)
            dve.drain().then_inc(s_dve, 1)
            chained[0] += 1
            dve.wait_ge(s_dve, chained[0])
            dve.tensor_scalar(localT[:, TILES:STEPS], localT[:, TILES:STEPS], NOWHERE, None, ALU.subtract)
            dve.drain().then_inc(s_steps, 1)

            def statistics(a):
                with dve.Fori(0, WINDOWS) as w:
                    dve.bn_stats(stats[:, ds(w, 1), :], a[:, ds(w, 1), :])
                link(dve.drain())
                half = stats[:, :, 0]
                link(dve.tensor_tensor(half, stats[:, :, 1], stats[:, :, 4], ALU.subtract))
                link(dve.tensor_tensor(half, half, half, ALU.mult))
                dve.tensor_tensor(mean[:, :], stats[:, :, 1], stats[:, :, 4], ALU.add)
                link(dve.tensor_tensor(stats[:, :, 2], stats[:, :, 2], stats[:, :, 5], ALU.add))
                link(dve.tensor_scalar(half, half, 0.25, None, ALU.mult))
                link(dve.tensor_scalar(mean[:, :], mean[:, :], 0.5, None, ALU.mult))
                dve.scalar_tensor_tensor(var[:, :], stats[:, :, 2], 1.0 / H, half,
                                         ALU.mult, ALU.add).then_inc(s_var, 1)

            def scales(roots, norms):
                dve.wait_ge(s_root, roots)
                link(dve.reciprocal(rstd[:, :], spread[:, :]))
                dve.scalar_tensor_tensor(shift[:, :], mean[:, :], -1.0, rstd[:, :],
                                         ALU.mult, ALU.mult).then_inc(s_scale, 1)

            dve.wait_ge(s_x, 32)
            statistics(X)
            scales(1, 1)

            with dve.Fori(0, TILES // BLOCK) as i:
                for j in range(BLOCK):
                    dve.wait_ge(s_deg, i * BLOCK + (j + DEG0 - RING + 1))
                    dve.tensor_scalar(msg[:, j % RING, 0:P], iota[:, :], digits[:, 0, ds(i * BLOCK + j, 1)],
                                      None, ALU.is_equal).then_inc(s_low, 1)
                    dve.tensor_scalar(hot[:, j % RING, 0:WINDOWS], iota[:, 0:WINDOWS],
                                      digits[:, 1, ds(i * BLOCK + j, 1)], wT[:, ds(i * BLOCK + j, 1)],
                                      ALU.is_equal, ALU.mult).then_inc(s_high, 1)
            dve.wait_ge(s_total, 1)
            degree = bank[7][:, 0:WINDOWS]
            link(dve.tensor_scalar(deg[:, 0, :], degree, 0.0, None, ALU.is_gt))
            link(dve.tensor_tensor(deg[:, 1, :], degree, deg[:, 0, :], ALU.mult))
            link(dve.scalar_tensor_tensor(deg[:, 1, :], deg[:, 1, :], 1.0, deg[:, 0, :], ALU.add, ALU.subtract))
            dve.drain().then_inc(s_var, 1)
            dve.wait_ge(s_root, 2)
            link(dve.reciprocal(dis[:, :], spread[:, :]))
            link(dve.tensor_tensor(dis[:, :], dis[:, :], deg[:, 0, :], ALU.mult))

            dve.wait_ge(s_h, WINDOWS)
            for g in range(GROUPS):
                ws = slice(g * GROUP, (g + 1) * GROUP)
                dve.tensor_tensor(T[:, ws, :], Hn[:, ws, :],
                                  dis[:, ws].unsqueeze(2).to_broadcast([P, GROUP, H]),
                                  ALU.mult).then_inc(s_scaled, 1)
            link(dve.tensor_tensor(X[:, :, :], X[:, :, :], Hn[:, :, :], ALU.add))
            link(dve.memset(S[:, :], 0.0))
            extras = dve.value_load(flags[0:1, 1:2])

            def sums(layer, lane_no):
                lane, first, count = LANES[lane_no]

                def build(i, j):
                    dve.wait_ge(lane.done, i * BLOCK + (layer * count + j + DONE0 - BLOCK + 1))
                    at = ds(i * BLOCK + (first + j), 1)
                    if layer < 2:
                        dve.tensor_scalar(hot[:, j, :], iota[:, :], localT[:, at], wT[:, at],
                                          ALU.is_equal, ALU.mult).then_inc(lane.hot, 1)
                    else:
                        dve.tensor_scalar(hot[:, j, :], iota[:, :], localT[:, at], None,
                                          ALU.is_equal).then_inc(lane.hot, 1)

                def scored(i, j):
                    dve.wait_ge(lane.z, i * BLOCK + (j + 1))
                    dve.scalar_tensor_tensor(junk[:, j % 2, :], bank[6 + j % 2][:, 0:H], 0.0, vec[:, 3, :],
                                             ALU.max, ALU.mult, accum_out=score[:, j % RING:j % RING + 1]
                                             ).then_inc(lane.scored, 1)

                bases = []

                def load_bases(i, j):
                    if j % RING == 0:
                        bases[:] = nc.values_load_multi_w_load_instructions(
                            baseT[0:1, ds(i * BLOCK + (first + j), RING)], engines=[mybir.EngineType.DVE],
                            min_val=0, max_val=SUMS - P)[1]

                def added(i, j):
                    dve.wait_ge(lane.done, i * BLOCK + (layer * count + j + DONE0 + 1))
                    dve.wait_ge(lane.added, i * BLOCK + (layer * count + j + ADDED0))
                    at = ds(bases[j % RING], P)
                    dve.tensor_tensor(S[:, at], S[:, at], bank[j % 4][:, 0:P], ALU.add).then_inc(lane.added, 1)

                sweep(dve, count // BLOCK, [(0, build)] + [(SCORE_LAG, scored)] * (layer == 2)
                      + [(ADD_LAG, load_bases), (ADD_LAG, added)])

            for layer in range(3):
                if layer == 2:
                    dve.wait_ge(s_tables, 16 * (3 * GROUPS + 1))
                    link(dve.memset(S[:, :], 0.0))
                    for g in range(GROUPS):
                        ws = slice(g * GROUP, (g + 1) * GROUP)
                        dve.tensor_tensor(X[:, ws, :], X[:, ws, :],
                                          vec[:, 5, :].unsqueeze(1).to_broadcast([P, GROUP, H]), ALU.add)
                sums(layer, 0)
                with dve.If(extras > 0):
                    dve.wait_ge(main.added, ADDED0 + (layer + 1) * TILES)
                    sums(layer, 1)
                if layer < 2:
                    dve.wait_ge(s_weights, 16 * 10)
                    with dve.Fori(0, GROUPS) as g:
                        for k in range(GROUP):
                            w = g * GROUP + k
                            dve.wait_ge(s_product, g * GROUP + (layer * WINDOWS + k + 1))
                            dve.scalar_tensor_tensor(T[:, ds(w, 1), :], bank[k][:, 0:H], dis[:, ds(w, 1)],
                                                     vec[:, layer, :], ALU.mult, ALU.add).then_inc(s_applied, 1)
                if layer == 0:
                    link(dve.memset(S[:, :], 0.0))
                if layer == 1:
                    link(dve.drain())
                    with dve.Fori(0, WINDOWS) as w:
                        dve.scalar_tensor_tensor(X[:, ds(w, 1), :], T[:, ds(w, 1), :], 0.0, X[:, ds(w, 1), :],
                                                 ALU.max, ALU.add)
                    link(dve.drain())
                    statistics(X)
                    scales(3, 2)
                    with dve.Fori(0, GROUPS) as g:
                        for k in range(GROUP):
                            w = g * GROUP + k
                            dve.wait_ge(s_ab, g * GROUP + (k + 1))
                            ab = bank[ab_bank(k)]
                            dve.tensor_tensor(T[:, ds(w, 1), :], ab[:, 0:H], vec[:, 2, :], ALU.add)
                            dve.tensor_copy(S[:, ds(w * H, H)], ab[:, H:2 * H]).then_inc(s_abread, 1)

            with dve.Fori(0, GROUPS) as g:
                for k in range(GROUP):
                    w = g * GROUP + k
                    dve.wait_ge(s_back, g * GROUP + (k + 1))
                    dve.tensor_tensor(Hn[:, ds(w, 1), :], bank[k][:, 0:P], Hn[:, ds(w, 1), :],
                                      ALU.add).then_inc(s_attended, 1)
            link(dve.drain())
            statistics(Hn)
            scales(4, 3)
            for g in range(GROUPS):
                ws = slice(g * GROUP, (g + 1) * GROUP)
                dve.wait_ge(s_normed, (g + 1) * GROUP)
                link(dve.tensor_tensor(T[:, ws, :], T[:, ws, :],
                                       vec[:, 4, :].unsqueeze(1).to_broadcast([P, GROUP, H]), ALU.mult))
                dve.tensor_tensor(T[:, ws, :], T[:, ws, :], X[:, ws, :], ALU.add).then_inc(s_final, 1)


_INS = ["x", "src", "dst", "edge_weight", "L0_gnn_W1", "L0_gnn_b1", "L0_gnn_W2", "L0_gnn_b2", "L1_gnn_W1",
        "L1_gnn_b1", "L1_gnn_W2", "L1_gnn_b2", "L1_gnn_gamma", "L1_gnn_beta"]


def kernel(**inputs):
    import numpy as np
    import concourse.bacc as bacc
    from concourse import mybir
    from concourse.bass_utils import run_bass_kernel_spmd as run

    nc = bacc.Bacc("TRN2", target_bir_lowering=False, num_devices=1)
    arrays, args = {}, []
    for name in _INS:
        a = np.ascontiguousarray(inputs[name])
        arrays[f"in_{name}"] = a
        args.append(nc.dram_tensor(f"in_{name}", a.shape, mybir.dt.from_np(a.dtype), kind="ExternalInput").ap())
    f32 = mybir.dt.float32
    args.append(nc.dram_tensor("out", (N, H), f32, kind="ExternalOutput").ap())
    for name, shape in (("rows1", (WINDOWS * P, H)), ("rows2", (WINDOWS * P, H)),
                        ("rows3", (WINDOWS * P, 2 * H)), ("brows", (SUMS, H))):
        args.append(nc.dram_tensor(name, shape, f32, kind="Internal").ap())
    args.append(nc.dram_tensor("records", (TILES * P, RECORD), mybir.dt.int32, kind="Internal").ap())
    gnn_kernel(nc, *args)
    r = run(nc, [arrays], core_ids=[0])
    return r.results[0]["out"]
```

```python
import concourse.bass as bass
from concourse import mybir
from contextlib import ExitStack


P = 128
N, H, E = 6250, 128, 100000
WINDOWS = -(-N // P)
LAST = N - (WINDOWS - 1) * P
BLOCK = 16
RING = 8
TILES = -(-E // (P * BLOCK)) * BLOCK
CHUNKS = 7
ROWS = TILES // CHUNKS
EXTRAS = -(-(N // P) // BLOCK) * BLOCK
STEPS = TILES + EXTRAS
SUMS = (N // P + 2) * P
GROUP = 7
GROUPS = WINDOWS // GROUP
FULL = E // (P * ROWS)
TAIL = E // P - FULL * ROWS
REST = E - (E // P) * P
NOWHERE = 16384.0
EPS = 1e-5
TURN_LAG, GATE_LAG, SCORE_LAG, OPEN_LAG, SUM_LAG, ADD_LAG = 1, 2, 3, 3, 6, 8
BASES = 8
RECORD = 4
SORT = 4
DIGIT = 7
STRIP, STRIPS = 32, 8
PACK = P // STRIP
BATCH = 16 * PACK
BATCHES = STEPS // BATCH
PLACES = PACK * (WINDOWS + 1)


def gnn_kernel(nc, x, src, dst, weight, g_w1, g_b1, g_w2, g_b2,
               a_w1, a_b1, a_w2, a_b2, gamma, beta, out, rows1, rows2, rows3, brows, records):
    f32, i32 = mybir.dt.float32, mybir.dt.int32
    ALU, ACT, AX = mybir.AluOpType, mybir.ActivationFunctionType, mybir.AxisListType
    ds = bass.ds

    ctx = ExitStack()
    with ctx:
        def sb(name, shape, dt=f32):
            return ctx.enter_context(nc.sbuf_tensor(name, shape, dt))

        def sem(name):
            return ctx.enter_context(nc.semaphore(name))

        bank = [ctx.enter_context(nc.psum_tensor(f"bank{i}", [P, 512], f32)) for i in range(8)]

        srcR = sb("srcR", [ROWS, CHUNKS, P], i32)
        dstR = sb("dstR", [ROWS, CHUNKS, P], i32)
        wR = sb("wR", [ROWS, CHUNKS, P])
        nextR = sb("nextR", [ROWS, CHUNKS, P], i32)
        srcF = sb("srcF", [ROWS, CHUNKS, P])
        dstF = sb("dstF", [ROWS, CHUNKS, P])
        localF = sb("localF", [ROWS, CHUNKS, P])
        cols = sb("cols", [ROWS, 9, CHUNKS])
        (VIOLATIONS,
         COUNT,
         TOTAL,
         THROUGH,
         UPTO,
         BEFORE,
         ORIGIN,
         SHIFT) = range(8)
        spanI = sb("spanI", [ROWS, 2, CHUNKS], i32)
        chosen = sb("chosen", [ROWS, CHUNKS, EXTRAS])
        srcT = sb("srcT", [P, STEPS], i32)
        localT = sb("localT", [P, STEPS])
        wT = sb("wT", [P, STEPS])
        baseT = sb("baseT", [1, STEPS], i32)
        baseF = sb("baseF", [1, STEPS])
        digitI = sb("digitI", [P, TILES], i32)
        digits = sb("digits", [P, TILES])
        flags = sb("flags", [1, 2], i32)

        iota = sb("iota", [P, P])
        ident = sb("ident", [P, P])
        upper = sb("upper", [P, P])
        ones = sb("ones", [P, P])
        zeros = sb("zeros", [P, P])
        W1 = sb("W1", [P, H])
        W2 = sb("W2", [P, H])
        AW = sb("AW", [P, 2, H])
        vec = sb("vec", [P, 6, H])
        ab2 = sb("ab2", [P, 1])

        X = sb("X", [P, WINDOWS, H])
        Hn = sb("Hn", [P, WINDOWS, H])
        T = sb("T", [P, WINDOWS, H])
        S = sb("S", [P, SUMS])
        stats = sb("stats", [P, WINDOWS, 6])
        mean = sb("mean", [P, WINDOWS])
        var = sb("var", [P, WINDOWS])
        rstd = sb("rstd", [P, WINDOWS])
        shift = sb("shift", [P, WINDOWS])
        deg = sb("deg", [P, 2, WINDOWS])
        spread = sb("spread", [P, WINDOWS])
        eps = sb("eps", [P, 1])
        dis = sb("dis", [P, WINDOWS])

        recF = T[:, 0:WINDOWS // 2 + 1, :].rearrange("p w f -> p (w f)")[:, 0:TILES * RECORD].rearrange(
            "p (t r) -> p t r", r=RECORD)
        recI = recF.bitcast(i32)
        strict = sb("strict", [P, P])
        moved = sb("moved", [P, SORT, RECORD], i32)
        place = sb("place", [P, SORT], i32)
        placeF = sb("placeF", [P, 1])
        counts = sb("counts", [P, 1])
        start = sb("start", [1, P])
        reached = sb("reached", [1, P])

        byStep = S[:, 0:6 * STEPS].rearrange("p (a s) -> p a s", s=STEPS)
        stepI = byStep[:, 0:2, :].bitcast(i32)
        stripI = byStep[:, 2:4, :].bitcast(i32)
        strip = byStep[:, 4, :]
        own = byStep[:, 5, :]
        target = sb("target", [P, BATCHES, PACK])
        offset = sb("offset", [P, 1])
        rowI = sb("rowI", [P, 3], i32)
        columns = sb("columns", [P, PLACES])
        sameStep = sb("sameStep", [P, PACK, STRIPS])
        sameGroup = sb("sameGroup", [P, 16, PACK])
        stack = sb("stack", [STRIP, PACK, P])
        strips = sb("strips", [STRIP, PLACES])

        picked = sb("picked", [P, 2, RING], i32)
        msg = sb("msg", [P, BLOCK, 2 * H])
        hot = sb("hot", [P, BLOCK, P])
        hotT = sb("hotT", [P, 4, P])
        gated = sb("gated", [P, 4, P])
        bwin = sb("bwin", [P, BLOCK, H])
        junk = sb("junk", [P, 2, P])
        score = sb("score", [P, RING])
        gate = sb("gate", [P, RING])

        ring1 = msg[:, :, :].rearrange("p s f -> p (s f)")
        ring2 = hot[:, :, :].rearrange("p s f -> p (s f)")
        ring3 = bwin[:, :, :].rearrange("p s f -> p (s f)")

        def placeHot(j):
            return ring1[:, j * BATCH * STRIP:(j + 1) * BATCH * STRIP]

        def stripHot(j):
            return ring2[:, j * BATCH * STRIPS:(j + 1) * BATCH * STRIPS]

        def masked(j):
            return ring2[:, (2 + j) * BATCH * STRIPS:(3 + j) * BATCH * STRIPS]

        def targetHot(j, t):
            return ring3[:, (j * PACK + t) * PLACES:(j * PACK + t + 1) * PLACES]

        def sumsOf(j):
            return gated[:, j, :]

        def swappedOf(j):
            return hotT[:, j, :]

        s_const = sem("s_const")
        s_in = sem("s_in")
        s_pad = sem("s_pad")
        s_weights = sem("s_weights")
        s_x = sem("s_x")
        s_xpad = sem("s_xpad")
        s_dve = sem("s_dve")
        s_pre = sem("s_pre")
        s_prep = sem("s_prep")
        s_flag = sem("s_flag")
        s_sclear = sem("s_sclear")
        s_sload = sem("s_sload")
        s_skeys = sem("s_skeys")
        s_shot = sem("s_shot")
        s_scount = sem("s_scount")
        s_stotal = sem("s_stotal")
        s_scounts = sem("s_scounts")
        s_sstart = sem("s_sstart")
        s_sstarted = sem("s_sstarted")
        s_smark = sem("s_smark")
        s_srank = sem("s_srank")
        s_splace = sem("s_splace")
        s_swrite = [sem(f"s_swrite{j}") for j in range(SORT)]
        s_sfree = sem("s_sfree")
        s_srows = sem("s_srows")
        s_steps = sem("s_steps")
        s_matched = sem("s_matched")
        s_batch = sem("s_batch")
        s_crossed = sem("s_crossed")
        s_masked = sem("s_masked")
        s_cut = sem("s_cut")
        s_swapped = sem("s_swapped")
        s_ready = sem("s_ready")
        s_strips = sem("s_strips")
        s_stacked = sem("s_stacked")
        s_total = sem("s_total")
        s_var = sem("s_var")
        s_root = sem("s_root")
        s_scale = sem("s_scale")
        s_stat = sem("s_stat")
        s_h = sem("s_h")
        s_scaled = sem("s_scaled")
        s_zeroed = sem("s_zeroed")
        s_product = sem("s_product")
        s_applied = sem("s_applied")
        s_rows = sem("s_rows")
        s_table = sem("s_table")
        s_added = sem("s_added")
        s_flip = sem("s_flip")
        s_flipped = sem("s_flipped")
        s_ab = sem("s_ab")
        s_abread = sem("s_abread")
        s_tables = sem("s_tables")
        s_back = sem("s_back")
        s_attended = sem("s_attended")
        s_normed = sem("s_normed")
        s_final = sem("s_final")
        s_issue = sem("s_issue")
        s_out = sem("s_out")

        class Lane:
            def __init__(self, tag):
                self.listed = [sem(f"listed{i}{tag}") for i in range(2)]
                self.gathered = [sem(f"gathered{i}{tag}") for i in range(BLOCK)]
                self.loaded = [sem(f"loaded{i}{tag}") for i in range(BLOCK)]
                self.hot = sem(f"hot{tag}")
                self.done = sem(f"done{tag}")
                self.added = sem(f"added{tag}")
                self.turned = sem(f"turned{tag}")
                self.hotT = sem(f"hotT{tag}")
                self.z = sem(f"z{tag}")
                self.scored = sem(f"scored{tag}")
                self.opened = sem(f"opened{tag}")
                self.gated = sem(f"gated{tag}")

        main, extra = Lane(""), Lane("x")
        LANES = ((main, 0, TILES), (extra, TILES, EXTRAS))
        DONE0, ADDED0, HOTT0, SCORED0 = 16, 8, 2, 2

        def sweep(engine, steps, stages, block=BLOCK):
            def place(i, j):
                for lag, do in stages:
                    before = (lag - j + block - 1) // block if lag > j else 0
                    if not isinstance(i, int) or 0 <= i * block + j - lag < steps:
                        do(i - before if before else i, j - lag + before * block)

            for j in range(block):
                place(0, j)
            with engine.Fori(1, steps // block) as i:
                for j in range(block):
                    place(i, j)
            for n in range(steps // block * block, steps + max(lag for lag, _ in stages)):
                place(n // block, n % block)

        def flip_bank(w):
            return w % GROUP % 3

        def ab_bank(w):
            return 3 + w % GROUP % 4

        block = ctx.enter_context(nc.Block())

        @block.sync
        def _(sp):
            def rows_of(a, first, rest):
                whole = first + FULL * ROWS * P
                tail = whole + TAIL * P
                return (a[first:whole].rearrange("(k q j) -> q k j", q=ROWS, j=P),
                        a[whole:tail].rearrange("(q j) -> q j", j=P),
                        a[tail:tail + rest].rearrange("(q j) -> q j", q=1))

            sp.wait_ge(s_pad, 1)
            for dest, a, first, rest in ((dstR, dst, 0, REST), (nextR, dst, 1, REST - 1),
                                         (srcR, src, 0, REST), (wR, weight, 0, REST)):
                whole, tail, last = rows_of(a, first, rest)
                sp.dma_start(dest[:, 0:FULL, :], whole).then_inc(s_in, 16)
                sp.dma_start(dest[0:TAIL, FULL, :], tail).then_inc(s_in, 16)
                sp.dma_start(dest[TAIL:TAIL + 1, FULL, 0:rest], last).then_inc(s_in, 16)
            sp.dma_start(X[:, 0:WINDOWS - 1, :],
                         x[0:(WINDOWS - 1) * P, :].rearrange("(w p) f -> p w f", p=P)).then_inc(s_x, 16)
            sp.wait_ge(s_xpad, 1)
            sp.dma_start(X[0:LAST, WINDOWS - 1, :], x[(WINDOWS - 1) * P:N, :]).then_inc(s_x, 16)
            sp.dma_start(W1[:, :], g_w1).then_inc(s_weights, 16)
            sp.dma_start(W2[:, :], g_w2).then_inc(s_weights, 16)
            sp.dma_start(AW[:, :, :], a_w1.rearrange("(k p) f -> p k f", p=P)).then_inc(s_weights, 16)
            for n, v in enumerate((g_b1, g_b2, a_b1, a_w2.rearrange("f o -> (f o)"), gamma, beta)):
                sp.dma_start(vec[:, n, :], v.unsqueeze(0).to_broadcast([P, H])).then_inc(s_weights, 16)
            sp.dma_start(ab2[:, :], a_b2.unsqueeze(0).to_broadcast([P, 1])).then_inc(s_weights, 16)

            def nodes(table, g, cols=slice(0, H)):
                return table[g * GROUP * P:(g + 1) * GROUP * P, cols].rearrange("(w p) f -> p w f", p=P)

            def group(a, g):
                return a[:, g * GROUP:(g + 1) * GROUP, :]

            sp.wait_ge(s_flag, 1)
            disorder = sp.value_load(flags[0:1, 0:1])
            with sp.If(disorder > 0), nc.allow_non_contiguous_dma(reason="edges out of order only"):
                sp.wait_ge(s_sclear, 1)
                whole = E // P * P
                for n, (a, rec) in enumerate(((src, recI), (dst, recI), (weight, recF))):
                    sp.dma_start(rec[:, 0:E // P, n], a[0:whole].rearrange("(t p) -> p t", p=P)
                                 ).then_inc(s_sload, 16)
                    sp.dma_start(rec[0:REST, E // P, n:n + 1], a[whole:E].rearrange("(p t) -> p t", t=1)
                                 ).then_inc(s_sload, 16)
                for j in range(SORT):
                    sp.wait_ge(s_swrite[j], 16 * (TILES // SORT))
                sp.dma_start(recI[:, :, :], records.rearrange("(t p) r -> p t r", p=P)).then_inc(s_sload, 16)
                for j in range(SORT):
                    sp.wait_ge(s_swrite[j], 2 * 16 * (TILES // SORT))
                for n, rows in enumerate((srcR, dstR, wR[:, :, :].bitcast(i32))):
                    for k in range(CHUNKS):
                        sp.dma_start(rows[:, k, :], records[k * ROWS * P:(k + 1) * ROWS * P, n].rearrange(
                            "(q j) -> q j", j=P)).then_inc(s_srows, 16)
            sp.wait_ge(s_steps, 1)
            extras = sp.value_load(flags[0:1, 1:2])

            def edges(layer, lane_no):
                lane, first, count = LANES[lane_no]
                blocks = count // BLOCK

                def indices(i, j):
                    if j % RING:
                        return
                    half = j // RING
                    if not (isinstance(i, int) and i + layer == 0):
                        for slot in range(half * RING, (half + 1) * RING):
                            sp.wait_ge(lane.gathered[slot], i * 16 + 16 * layer * blocks)
                    sp.dma_start(picked[:, half, :], srcT[:, ds(i * BLOCK + (first + j), RING)]
                                 ).then_inc(lane.listed[half], 16)

                bases = []

                def rows(i, j):
                    if j == 0:
                        bases[:] = nc.values_load_multi_w_load_instructions(
                            baseT[0:1, ds(i * BLOCK + first, BLOCK)], engines=[mybir.EngineType.SP],
                            min_val=0, max_val=SUMS - P)[1]
                    base = bases[j]
                    sp.wait_ge(lane.done, i * BLOCK + (layer * count + j + DONE0 - BLOCK + 1))
                    sp.dma_start(bwin[:, j, :], brows[ds(base, P), :]).then_inc(lane.loaded[j], 16)

                sweep(sp, count, [(0, indices)] + [(0, rows)] * (layer == 2))

            for layer in range(3):
                if layer == 0:
                    for g in range(GROUPS):
                        sp.wait_ge(s_scaled, g + 1)
                        sp.dma_start(nodes(rows1, g), group(T, g)).then_inc(s_table, 16)
                elif layer == 1:
                    for g in range(GROUPS):
                        sp.wait_ge(s_rows, (g + 1) * GROUP)
                        sp.dma_start(nodes(rows2, g), group(T, g)).then_inc(s_table, 16)
                else:
                    for g in range(GROUPS):
                        sp.wait_ge(s_abread, (g + 1) * GROUP)
                        sp.dma_start(nodes(rows3, g), group(Hn, g)).then_inc(s_tables, 16)
                        sp.dma_start(nodes(rows3, g, slice(H, 2 * H)), group(T, g)).then_inc(s_tables, 16)
                        sp.dma_start(nodes(brows, g), S[:, g * GROUP * P:(g + 1) * GROUP * P].rearrange(
                            "p (w f) -> p w f", f=H)).then_inc(s_tables, 16)
                    sp.dma_start(brows[WINDOWS * P:SUMS, :], zeros[:, :]).then_inc(s_tables, 16)
                    sp.wait_ge(s_tables, 16 * (3 * GROUPS + 1))
                edges(layer, 0)
                with sp.If(extras > 0):
                    sp.wait_ge(main.done, DONE0 + (layer + 1) * TILES)
                    edges(layer, 1)

            for g in range(GROUPS):
                sp.wait_ge(s_final, g + 1)
                full = GROUP if g < GROUPS - 1 else GROUP - 1
                w0 = g * GROUP
                sp.dma_start(out[w0 * P:(w0 + full) * P, :].rearrange("(w p) f -> p w f", p=P),
                             T[:, w0:w0 + full, :]).then_inc(s_out, 16)
            sp.dma_start(out[(WINDOWS - 1) * P:N, :], T[0:LAST, WINDOWS - 1, :]).then_inc(s_out, 16)
            sp.wait_ge(s_out, 16 * (GROUPS + 1))

        @block.gpsimd
        def _(pool):
            pool.memset(ones[:, :], 1.0).then_inc(s_const, 1)
            pool.memset(zeros[:, :], 0.0).then_inc(s_const, 1)
            pool.iota(iota[:, :], [[1, P]], base=0, channel_multiplier=0,
                      allow_small_or_imprecise_dtypes=True).then_inc(s_const, 1)
            pool.wait_ge(s_const, 3)
            pool.affine_select(out=ident[:, :], in_=ones[:, :], pattern=[[1, P]], compare_op=ALU.is_equal,
                               fill=0.0, base=0, channel_multiplier=-1).then_inc(s_const, 1)
            pool.affine_select(out=strict[:, :], in_=ones[:, :], pattern=[[1, P]], compare_op=ALU.is_gt,
                               fill=0.0, base=0, channel_multiplier=-1).then_inc(s_const, 1)
            pool.affine_select(out=upper[:, :], in_=ones[:, :], pattern=[[1, P]], compare_op=ALU.is_ge,
                               fill=0.0, base=0, channel_multiplier=-1).then_inc(s_const, 1)
            pool.iota(columns[:, :], [[1, PLACES]], base=0, channel_multiplier=0,
                      allow_small_or_imprecise_dtypes=True).then_inc(s_const, 1)
            pool.iota(rowI[:, 0:1], [[0, 1]], base=0, channel_multiplier=1).then_inc(s_const, 1)
            for kept, size, inner in ((sameStep, STRIP, STRIPS), (sameGroup, STRIPS, PACK)):
                count = P // size
                pool.affine_select(out=kept[:, :, :], in_=ones[:, 0:count * inner].rearrange(
                    "p (a b) -> p a b", b=inner), pattern=[[-size, count], [0, inner]], compare_op=ALU.is_ge,
                    fill=0.0, base=0, channel_multiplier=1).then_inc(s_const, 1)
            pool.wait_ge(s_const, 10)
            for kept, size, inner in ((sameStep, STRIP, STRIPS), (sameGroup, STRIPS, PACK)):
                pool.affine_select(out=kept[:, :, :], in_=kept[:, :, :],
                                   pattern=[[size, P // size], [0, inner]], compare_op=ALU.is_ge,
                                   fill=0.0, base=size - 1, channel_multiplier=-1).then_inc(s_const, 1)
            for q in range(PACK):
                pool.affine_select(out=stack[:, q, :], in_=ones[0:STRIP, :], pattern=[[1, P]],
                                   compare_op=ALU.is_equal, fill=0.0, base=-STRIP * q,
                                   channel_multiplier=-1).then_inc(s_const, 1)
            pool.wait_ge(s_flag, 1)
            disorder = pool.value_load(flags[0:1, 0:1])
            with pool.If(disorder > 0):
                for digit in range(2):
                    if digit == 1:
                        pool.wait_ge(s_sload, 16 * 7)
                    with pool.Fori(0, TILES // SORT) as i:
                        for j in range(SORT):
                            pool.wait_ge(s_splace, i * SORT + (digit * TILES + j + 1))
                            pool.sem_inc(s_issue, 1)
                            pool.indirect_dma_start(
                                out=records[:, :], out_offset=bass.IndirectOffsetOnAxis(ap=place[:, j:j + 1], axis=0),
                                in_=moved[:, j, :], in_offset=None).then_inc(s_swrite[j], 16)
                        for j in range(SORT):
                            pool.wait_ge(s_swrite[j], i * 16 + 16 * (digit * (TILES // SORT) + 1))
                        pool.sem_inc(s_sfree, SORT)
            pool.wait_ge(s_steps, 1)
            extras = pool.value_load(flags[0:1, 1:2])

            def gathers(layer, lane_no):
                lane, first, count = LANES[lane_no]
                table, width = ((rows1, H), (rows2, H), (rows3, 2 * H))[layer]
                def gather(i, j):
                    half = j // RING
                    if j % RING == 0:
                        pool.wait_ge(lane.listed[half], i * 16 + 16 * (layer * (count // BLOCK) + 1))
                    if j % 4 == 0:
                        pool.wait_ge(lane.done, i * BLOCK + (layer * count + j + 3 + DONE0 - BLOCK + 1))
                        pool.sem_inc(s_issue, 1)
                    pool.indirect_dma_start(
                        out=msg[:, j, 0:width], out_offset=None, in_=table[:, :],
                        in_offset=bass.IndirectOffsetOnAxis(ap=picked[:, half, j % RING:j % RING + 1], axis=0),
                    ).then_inc(lane.gathered[j], 16)

                with pool.Fori(0, count // BLOCK) as i:
                    for j in range(BLOCK):
                        gather(i, j)

            for layer in range(3):
                if layer < 2:
                    pool.wait_ge(s_table, 16 * GROUPS * (layer + 1))
                else:
                    pool.wait_ge(s_tables, 16 * (3 * GROUPS + 1))
                gathers(layer, 0)
                with pool.If(extras > 0):
                    pool.wait_ge(main.done, DONE0 + (layer + 1) * TILES)
                    gathers(layer, 1)

        @block.tensor
        def _(pe):
            pe.sem_inc(main.done, DONE0)
            pe.sem_inc(extra.done, DONE0)
            pe.wait_ge(s_const, 6)
            pe.wait_ge(s_pre, 1)
            pe.matmul(bank[0][:, 0:1], ones[0:ROWS, :], cols[0:ROWS, VIOLATIONS, 0:1],
                      start=True, stop=True).then_inc(s_prep, 1)

            pe.wait_ge(s_flag, 1)
            disorder = pe.value_load(flags[0:1, 0:1])
            with pe.If(disorder > 0):
                pe.sem_inc(s_scount, SORT)
                for digit in range(2):
                    pe.matmul(bank[0][:, 0:1], zeros[:, :], zeros[:, 0:1], start=True, stop=False,
                              skip_group_check=True)
                    with pe.Fori(0, TILES // SORT) as i:
                        for j in range(SORT):
                            pe.wait_ge(s_shot, i * SORT + (digit * TILES + j + 1))
                            pe.matmul(bank[0][:, 0:1], hot[:, j, :], ones[:, 0:1], start=False, stop=False,
                                      skip_group_check=True).then_inc(s_scount, 1)
                    pe.matmul(bank[0][:, 0:1], zeros[:, :], zeros[:, 0:1], start=False, stop=True,
                              skip_group_check=True).then_inc(s_stotal, 1)
                    pe.wait_ge(s_scounts, digit + 1)
                    pe.matmul(bank[1][0:1, 0:P], counts[:, :], strict[:, :], start=True, stop=True
                              ).then_inc(s_sstart, 1)
                    pe.wait_ge(s_sstarted, digit + 1)
                    pe.matmul(bank[3][0:1, 0:P], ones[0:1, 0:1], start[:, :], start=True, stop=False,
                              skip_group_check=True)
                    with pe.Fori(0, TILES // SORT) as i:
                        for j in range(SORT):
                            pe.wait_ge(s_smark, i * SORT + (digit * TILES + j + 1))
                            pe.matmul(bank[2][:, 0:P], strict[:, :], hot[:, 8 + j, :], start=True, stop=False)
                            pe.matmul(bank[2][:, 0:P], ones[0:1, :], reached[:, :], start=False, stop=True)
                            pe.matmul(bank[3][0:1, 0:P], ones[:, 0:1], hot[:, 8 + j, :], start=False, stop=False,
                                      skip_group_check=True).then_inc(s_srank, 1)
                    pe.wait_ge(s_splace, (digit + 1) * TILES)
                    pe.matmul(bank[3][0:1, 0:P], zeros[:, 0:1], zeros[:, :], start=False, stop=True,
                              skip_group_check=True)

            pe.wait_ge(s_pre, 2)
            pe.matmul(bank[1][0:ROWS, 0:CHUNKS], upper[0:ROWS, 0:ROWS], cols[0:ROWS, COUNT, :],
                      start=True, stop=True).then_inc(s_prep, 1)
            pe.matmul(bank[2][:, 0:CHUNKS], ones[0:ROWS, :], cols[0:ROWS, COUNT, :],
                      start=True, stop=True).then_inc(s_prep, 1)
            pe.wait_ge(s_pre, 3)
            for a, rows in enumerate((srcF, localF, wR, dstF)):
                for k in range(CHUNKS):
                    last = pe.transpose(bank[2 * a + k // 4][:, (k % 4) * ROWS:(k % 4 + 1) * ROWS],
                                        rows[:, k, :], ident[0:ROWS, 0:ROWS])
                last.then_inc(s_prep, 1)
            pe.wait_ge(s_pre, 4)
            for a, rows in enumerate((srcF, localF, wR)):
                for k in range(CHUNKS):
                    last = pe.matmul(bank[a][:, 0:EXTRAS], rows[:, k, :], chosen[:, k, :],
                                     start=(k == 0), stop=(k == CHUNKS - 1))
                last.then_inc(s_prep, 1)
            for k in range(CHUNKS):
                last = pe.matmul(bank[3][0:1, 0:EXTRAS], cols[0:ROWS, ORIGIN, k:k + 1], chosen[:, k, :],
                                 start=(k == 0), stop=(k == CHUNKS - 1))
            last.then_inc(s_prep, 1)

            pe.wait_ge(s_pre, 5)
            for half in range(2):
                last = pe.matmul(bank[6 + half][:, 0:STEPS // 2], ones[0:1, :],
                                 baseF[:, half * (STEPS // 2):(half + 1) * (STEPS // 2)], start=True, stop=True)
            last.then_inc(s_prep, 1)

            def crossed(i, j):
                pe.wait_ge(s_batch, i * 2 + (j + 1))
                for g in range(16):
                    last = pe.matmul(bank[j][:, g * P // 4:(g + 1) * P // 4], placeHot(j)[:, g * P:(g + 1) * P],
                                     stripHot(j)[:, g * P // 4:(g + 1) * P // 4], start=True, stop=True)
                last.then_inc(s_crossed, 1)

            def swapped(i, j):
                pe.wait_ge(s_cut, i * 2 + (j + 1))
                pe.transpose(bank[2 + j][:, 0:P], sumsOf(j), ident[:, :]).then_inc(s_swapped, 1)

            def placed(i, j):
                pe.wait_ge(s_ready, i * 2 + (j + 1))
                for t in range(PACK):
                    pe.matmul(bank[4][0:STRIP, 0:PLACES], swappedOf(j)[:, t * STRIP:(t + 1) * STRIP],
                              targetHot(j, t), start=False, stop=False, skip_group_check=True)

            pe.wait_ge(s_const, 16)
            pe.matmul(bank[4][0:STRIP, 0:PLACES], zeros[:, 0:STRIP], columns[:, :], start=True, stop=False,
                      skip_group_check=True)
            sweep(pe, BATCHES, [(0, crossed), (1, swapped), (2, placed)], block=2)
            pe.matmul(bank[4][0:STRIP, 0:PLACES], zeros[:, 0:STRIP], columns[:, :], start=False, stop=True,
                      skip_group_check=True).then_inc(s_strips, 1)
            pe.wait_ge(s_stacked, 1)
            for q in range(PACK):
                last = pe.matmul(bank[5][:, 0:WINDOWS], stack[:, q, :],
                                 strips[:, q * (WINDOWS + 1):q * (WINDOWS + 1) + WINDOWS],
                                 start=(q == 0), stop=(q == PACK - 1))
            last.then_inc(s_total, 1)
            extras = pe.value_load(flags[0:1, 1:2])

            def products(layer, lane_no):
                lane, first, count = LANES[lane_no]
                blocks = count // BLOCK

                def rows_here(i, j):
                    pe.wait_ge(lane.gathered[j], i * 16 + 16 * (layer * blocks + 1))

                def bank_free(i, j):
                    pe.wait_ge(lane.added, i * BLOCK + (layer * count + j + ADDED0 - 4 + 1))

                def summed(i, j):
                    rows_here(i, j)
                    pe.wait_ge(lane.hot, i * BLOCK + (layer * count + j + 1))
                    bank_free(i, j)
                    pe.matmul(bank[j % 4][:, 0:P], msg[:, j, 0:H], hot[:, j, :],
                              start=True, stop=True).then_inc(lane.done, 1)

                def turn(i, j):
                    pe.wait_ge(lane.hot, i * BLOCK + (layer * count + j + 1))
                    pe.wait_ge(lane.hotT, i * BLOCK + (j + HOTT0 - 2 + 1))
                    pe.transpose(bank[4 + j % 2][:, 0:P], hot[:, j, :],
                                 ident[:, :]).then_inc(lane.turned, 1)

                def gate_input(i, j):
                    rows_here(i, j)
                    pe.wait_ge(lane.loaded[j], i * 16 + 16)
                    pe.wait_ge(lane.hotT, i * BLOCK + (j + HOTT0 + 1))
                    pe.wait_ge(lane.scored, i * BLOCK + (j + SCORED0 - 2 + 1))
                    pe.matmul(bank[6 + j % 2][:, 0:H], hotT[:, j % 4, :], bwin[:, j, :],
                              start=True, stop=False)
                    pe.matmul(bank[6 + j % 2][:, 0:H], ident[:, :], msg[:, j, H:2 * H],
                              start=False, stop=True).then_inc(lane.z, 1)

                def gated_sum(i, j):
                    pe.wait_ge(lane.gated, i * BLOCK + (j + 1))
                    bank_free(i, j)
                    pe.matmul(bank[j % 4][:, 0:P], msg[:, j, 0:H], gated[:, j % 4, :],
                              start=True, stop=True).then_inc(lane.done, 1)

                if layer < 2:
                    sweep(pe, count, [(0, summed)])
                else:
                    sweep(pe, count, [(TURN_LAG, turn), (GATE_LAG, gate_input), (SUM_LAG, gated_sum)])

            def earlier(w, slot):
                same = [v for v in range(w) if slot(v) == slot(w)]
                return same[-1] if same else None

            for layer in range(3):
                if layer == 2:
                    pe.wait_ge(s_abread, WINDOWS)
                products(layer, 0)
                with pe.If(extras > 0):
                    pe.wait_ge(main.added, ADDED0 + (layer + 1) * TILES)
                    products(layer, 1)
                if layer < 2:
                    pe.wait_ge(s_weights, 16 * 10)
                    pe.wait_ge(main.added, ADDED0 + (layer + 1) * TILES)
                    with pe.If(extras > 0):
                        pe.wait_ge(extra.added, ADDED0 + (layer + 1) * EXTRAS)
                    for w in range(WINDOWS):
                        n = layer * WINDOWS + w
                        if n >= GROUP:
                            pe.wait_ge(s_applied, n - GROUP + 1)
                        pe.matmul(bank[w % GROUP][:, 0:H], S[:, w * P:(w + 1) * P], (W1, W2)[layer][:, :],
                                  start=True, stop=True).then_inc(s_product, 1)
                if layer == 1:
                    pe.wait_ge(s_applied, 2 * WINDOWS)
                    for w in range(WINDOWS + 1):
                        if w < WINDOWS:
                            pe.wait_ge(s_h, WINDOWS + w + 1)
                            v = earlier(w, flip_bank)
                            if v is not None:
                                pe.wait_ge(s_flipped, v + 1)
                            pe.transpose(bank[flip_bank(w)][:, 0:P], Hn[:, w, :],
                                         ident[:, :]).then_inc(s_flip, 1)
                        if w >= 1:
                            u = w - 1
                            pe.wait_ge(s_flipped, u + 1)
                            v = earlier(u, ab_bank)
                            if v is not None:
                                pe.wait_ge(s_abread, v + 1)
                            pe.matmul(bank[ab_bank(u)][:, 0:2 * H], hot[:, u % GROUP, :],
                                      AW[:, :, :].rearrange("p k f -> p (k f)"),
                                      start=True, stop=True).then_inc(s_ab, 1)
                if layer == 2:
                    pe.wait_ge(main.added, ADDED0 + 3 * TILES)
                    with pe.If(extras > 0):
                        pe.wait_ge(extra.added, ADDED0 + 3 * EXTRAS)
                    for w in range(WINDOWS):
                        if w >= GROUP:
                            pe.wait_ge(s_attended, w - GROUP + 1)
                        pe.transpose(bank[w % GROUP][:, 0:P], S[:, w * P:(w + 1) * P],
                                     ident[:, :]).then_inc(s_back, 1)

        @block.scalar
        def _(act):
            for lane in (main, extra):
                act.sem_inc(lane.hotT, HOTT0)
            act.wait_ge(s_var, 1)
            act.activation(spread[:, :], var[:, :], ACT.Sqrt, bias=eps[:, 0:1]).then_inc(s_root, 1)
            act.wait_ge(s_scale, 1)
            with act.Fori(0, WINDOWS) as w:
                act.activation(Hn[:, ds(w, 1), :], X[:, ds(w, 1), :], ACT.Relu, bias=shift[:, ds(w, 1)],
                               scale=rstd[:, ds(w, 1)]).then_inc(s_h, 1)
            act.wait_ge(s_var, 2)
            act.activation(spread[:, :], deg[:, 1, :], ACT.Sqrt).then_inc(s_root, 1)
            act.wait_ge(s_steps, 1)
            extras = act.value_load(flags[0:1, 1:2])

            with act.Fori(0, WINDOWS) as w:
                act.wait_ge(s_applied, w + 1)
                act.activation(T[:, ds(w, 1), :], T[:, ds(w, 1), :], ACT.Relu,
                               scale=dis[:, ds(w, 1)]).then_inc(s_rows, 1)

            act.wait_ge(s_var, 3)
            act.activation(spread[:, :], var[:, :], ACT.Sqrt, bias=eps[:, 0:1]).then_inc(s_root, 1)
            act.wait_ge(s_scale, 2)
            with act.Fori(0, WINDOWS) as w:
                act.activation(Hn[:, ds(w, 1), :], X[:, ds(w, 1), :], ACT.Relu, bias=shift[:, ds(w, 1)],
                               scale=rstd[:, ds(w, 1)]).then_inc(s_h, 1)
            with act.Fori(0, GROUPS) as g:
                for k in range(GROUP):
                    act.wait_ge(s_flip, g * GROUP + (k + 1))
                    act.activation(hot[:, k, :], bank[flip_bank(k)][:, 0:P], ACT.Copy).then_inc(s_flipped, 1)

            def gates(lane_no):
                lane, first, count = LANES[lane_no]

                def copy(i, j):
                    act.wait_ge(lane.turned, i * BLOCK + (j + 1))
                    act.activation(hotT[:, j % 4, :], bank[4 + j % 2][:, 0:P], ACT.Copy).then_inc(lane.hotT, 1)

                def opened(i, j):
                    act.wait_ge(lane.scored, i * BLOCK + (j + SCORED0 + 1))
                    act.activation(gate[:, j % RING:j % RING + 1], score[:, j % RING:j % RING + 1],
                                   ACT.Sigmoid, bias=ab2[:, 0:1]).then_inc(lane.opened, 1)

                def times(i, j):
                    act.wait_ge(lane.opened, i * BLOCK + (j + 1))
                    act.wait_ge(lane.done, i * BLOCK + (2 * count + j + DONE0 - 4 + 1))
                    act.activation(gated[:, j % 4, :], hot[:, j, :], ACT.Copy,
                                   scale=gate[:, j % RING:j % RING + 1]).then_inc(lane.gated, 1)

                sweep(act, count, [(TURN_LAG, copy), (OPEN_LAG, opened), (OPEN_LAG + 1, times)])

            gates(0)
            with act.If(extras > 0):
                gates(1)

            act.wait_ge(s_var, 4)
            act.activation(spread[:, :], var[:, :], ACT.Sqrt, bias=eps[:, 0:1]).then_inc(s_root, 1)
            act.wait_ge(s_scale, 3)
            with act.Fori(0, WINDOWS) as w:
                act.activation(T[:, ds(w, 1), :], Hn[:, ds(w, 1), :], ACT.Identity, bias=shift[:, ds(w, 1)],
                               scale=rstd[:, ds(w, 1)]).then_inc(s_normed, 1)

        @block.vector
        def _(dve):
            chained = [0]

            def link(ins):
                chained[0] += 1
                ins.then_inc(s_dve, 1)
                dve.wait_ge(s_dve, chained[0])

            for lane in (main, extra):
                dve.sem_inc(lane.added, ADDED0)
                dve.sem_inc(lane.scored, SCORED0)
            dve.memset(dstR[:, FULL, :], N)
            dve.memset(nextR[:, FULL, :], N)
            dve.memset(srcR[:, FULL, :], 0)
            link(dve.memset(wR[:, FULL, :], 0.0))
            dve.drain().then_inc(s_pad, 1)
            dve.memset(eps[:, :], EPS)
            dve.memset(X[:, WINDOWS - 1, :], 0.0).then_inc(s_xpad, 1)

            def col(n):
                return cols[0:ROWS, n, :]

            dve.wait_ge(s_in, 16 * 12)
            dve.wait_ge(s_const, 6)
            link(dve.tensor_tensor(srcF[:, :, :], nextR[:, :, :], dstR[:, :, :], ALU.is_lt))
            link(dve.tensor_reduce(col(VIOLATIONS), srcF[:, :, :], AX.X, ALU.add))
            link(dve.tensor_reduce(cols[0:ROWS, VIOLATIONS, 0:1], col(VIOLATIONS), AX.X, ALU.add))
            dve.drain().then_inc(s_pre, 1)
            dve.wait_ge(s_prep, 1)
            link(dve.tensor_copy(flags[0:1, 0:1], bank[0][0:1, 0:1]))
            dve.drain().then_inc(s_flag, 1)
            disorder = dve.value_load(flags[0:1, 0:1])
            with dve.If(disorder > 0):
                dve.sem_inc(s_sfree, SORT)
                dve.memset(recI[:, :, :], 0)
                dve.drain()
                dve.memset(recI[:, E // P:TILES, 1], N)
                dve.drain().then_inc(s_sclear, 1)
                for digit in range(2):
                    dve.wait_ge(s_sload, 16 * (6 + digit))
                    dve.tensor_scalar(digitI[:, :], recI[:, :, 1], (P - 1, DIGIT)[digit], None,
                                      (ALU.bitwise_and, ALU.logical_shift_right)[digit])
                    dve.drain()
                    dve.tensor_copy(digits[:, :], digitI[:, :])
                    dve.drain()
                    with dve.Fori(0, TILES // SORT) as i:
                        for j in range(SORT):
                            dve.wait_ge(s_scount, i * SORT + (digit * TILES + j + 1))
                            dve.tensor_scalar(hot[:, j, :], iota[:, :], digits[:, ds(i * SORT + j, 1)],
                                              None, ALU.is_equal).then_inc(s_shot, 1)
                    dve.wait_ge(s_stotal, digit + 1)
                    dve.tensor_copy(counts[:, :], bank[0][:, 0:1]).then_inc(s_scounts, 1)
                    dve.wait_ge(s_sstart, digit + 1)
                    dve.tensor_copy(start[:, :], bank[1][0:1, 0:P])
                    dve.tensor_copy(reached[:, :], bank[1][0:1, 0:P])
                    dve.drain().then_inc(s_sstarted, 1)
                    with dve.Fori(0, TILES // SORT) as i:
                        for j in range(SORT):
                            t = i * SORT + j
                            dve.tensor_scalar(hot[:, 8 + j, :], iota[:, :], digits[:, ds(t, 1)],
                                              None, ALU.is_equal).then_inc(s_smark, 1)
                            if j == 0:
                                dve.wait_ge(s_sfree, i * SORT + (digit * TILES + SORT))
                            dve.tensor_copy(moved[:, j, :], recI[:, ds(t, 1), :].rearrange("p t r -> p (t r)"))
                            dve.wait_ge(s_srank, i * SORT + (digit * TILES + j + 1))
                            dve.scalar_tensor_tensor(junk[:, 0, :], bank[2][:, 0:P], 1.0, hot[:, 8 + j, :],
                                                     ALU.mult, ALU.mult, accum_out=placeF[:, 0:1])
                            dve.tensor_copy(reached[:, :], bank[3][0:1, 0:P])
                            dve.drain()
                            dve.tensor_copy(place[:, j:j + 1], placeF[:, :]).then_inc(s_splace, 1)
                dve.wait_ge(s_srows, 16 * 3 * CHUNKS)
            dve.tensor_copy(srcF[:, :, :], srcR[:, :, :])
            link(dve.tensor_copy(dstF[:, :, :], dstR[:, :, :]))
            for k in range(CHUNKS):
                dve.tensor_scalar(localF[:, k, :], dstF[:, k, :], dstF[:, k, 0:1], None, ALU.subtract)
            link(dve.tensor_tensor(spanI[:, 0, :], dstR[:, :, P - 1], dstR[:, :, 0], ALU.subtract))
            link(dve.tensor_scalar(spanI[:, 1, :], spanI[:, 0, :], DIGIT, None, ALU.arith_shift_right))
            link(dve.tensor_copy(col(COUNT), spanI[:, 1, :]))
            dve.drain().then_inc(s_pre, 1)
            dve.wait_ge(s_prep, 3)
            link(dve.tensor_copy(col(TOTAL), bank[2][0:ROWS, 0:CHUNKS]))
            link(dve.tensor_tensor_scan(col(THROUGH), ones[0:ROWS, 0:CHUNKS], col(TOTAL), 0.0, ALU.mult, ALU.add))
            link(dve.tensor_copy(flags[0:1, 1:2], cols[0:1, THROUGH, CHUNKS - 1:CHUNKS]))
            link(dve.tensor_tensor(col(THROUGH), col(THROUGH), col(TOTAL), ALU.subtract))
            link(dve.tensor_tensor(col(UPTO), bank[1][0:ROWS, 0:CHUNKS], col(THROUGH), ALU.add))
            dve.drain().then_inc(s_pre, 1)
            link(dve.tensor_tensor(col(BEFORE), col(UPTO), col(COUNT), ALU.subtract))
            link(dve.tensor_scalar(col(ORIGIN), col(BEFORE), -float(P), float(P), ALU.mult, ALU.add))
            dve.tensor_scalar(col(SHIFT), col(ORIGIN), -1.0, NOWHERE, ALU.mult, ALU.add)
            link(dve.tensor_tensor(col(ORIGIN), col(ORIGIN), dstF[:, :, 0], ALU.add))

            banks4 = 4 * ROWS
            for a, dest in enumerate((srcT, localT, wT, baseF)):
                dve.wait_ge(s_prep, 4 + a)
                lines = 1 if a == 3 else P
                dve.tensor_copy(dest[:, 0:banks4], bank[2 * a][0:lines, 0:banks4])
                link(dve.tensor_copy(dest[:, banks4:TILES], bank[2 * a + 1][0:lines, 0:TILES - banks4]))

            for k in range(CHUNKS):
                link(dve.tensor_scalar(chosen[:, k, :], iota[0:ROWS, 0:EXTRAS], cols[0:ROWS, UPTO, k:k + 1],
                                       None, ALU.is_lt))
                link(dve.scalar_tensor_tensor(chosen[:, k, :], iota[0:ROWS, 0:EXTRAS],
                                              cols[0:ROWS, BEFORE, k:k + 1], chosen[:, k, :],
                                              ALU.is_ge, ALU.mult))
                link(dve.tensor_scalar(localF[:, k, :], localF[:, k, :], cols[0:ROWS, SHIFT, k:k + 1],
                                       None, ALU.add))
            dve.drain().then_inc(s_pre, 1)
            dve.wait_ge(s_const, 16)
            dve.tensor_scalar(rowI[:, 1:2], rowI[:, 0:1], PACK - 1, None, ALU.bitwise_and)
            link(dve.tensor_scalar(rowI[:, 2:3], rowI[:, 0:1], 2, 1, ALU.logical_shift_right, ALU.bitwise_and))
            dve.scalar_tensor_tensor(offset[:, :], rowI[:, 1:2], float(WINDOWS + 1), rowI[:, 2:3],
                                     ALU.mult, ALU.add)
            dve.wait_ge(s_prep, 11)
            dve.tensor_copy(srcT[:, TILES:STEPS], bank[0][:, 0:EXTRAS])
            dve.scalar_tensor_tensor(localT[:, TILES:STEPS], iota[:, 0:EXTRAS], -float(P),
                                     bank[1][:, 0:EXTRAS], ALU.mult, ALU.add)
            dve.tensor_copy(wT[:, TILES:STEPS], bank[2][:, 0:EXTRAS])
            dve.scalar_tensor_tensor(baseF[0:1, TILES:STEPS], iota[0:1, 0:EXTRAS], float(P),
                                     bank[3][0:1, 0:EXTRAS], ALU.mult, ALU.add)
            dve.drain().then_inc(s_dve, 1)
            chained[0] += 1
            dve.wait_ge(s_dve, chained[0])
            dve.sem_inc(s_pre, 1)
            dve.tensor_scalar(localT[:, TILES:STEPS], localT[:, TILES:STEPS], NOWHERE, None, ALU.subtract)
            dve.tensor_copy(baseT[:, :], baseF[:, :])
            dve.drain().then_inc(s_steps, 1)

            def statistics(a):
                with dve.Fori(0, GROUPS) as g:
                    for k in range(GROUP):
                        w = ds(g * GROUP + k, 1)
                        dve.bn_stats(stats[:, w, :], a[:, w, :])
                link(dve.drain())
                half = stats[:, :, 0]
                link(dve.tensor_tensor(half, stats[:, :, 1], stats[:, :, 4], ALU.subtract))
                link(dve.tensor_tensor(half, half, half, ALU.mult))
                dve.tensor_tensor(mean[:, :], stats[:, :, 1], stats[:, :, 4], ALU.add)
                link(dve.tensor_tensor(stats[:, :, 2], stats[:, :, 2], stats[:, :, 5], ALU.add))
                link(dve.tensor_scalar(half, half, 0.25, None, ALU.mult))
                link(dve.tensor_scalar(mean[:, :], mean[:, :], 0.5, None, ALU.mult))
                dve.scalar_tensor_tensor(var[:, :], stats[:, :, 2], 1.0 / H, half,
                                         ALU.mult, ALU.add).then_inc(s_var, 1)

            def scales(roots, norms):
                dve.wait_ge(s_root, roots)
                link(dve.reciprocal(rstd[:, :], spread[:, :]))
                dve.scalar_tensor_tensor(shift[:, :], mean[:, :], -1.0, rstd[:, :],
                                         ALU.mult, ALU.mult).then_inc(s_scale, 1)

            dve.wait_ge(s_x, 32)
            statistics(X)
            scales(1, 1)

            dve.wait_ge(s_prep, 12)
            for half in range(2):
                at = slice(half * (STEPS // 2), (half + 1) * (STEPS // 2))
                dve.tensor_tensor(stepI[:, 0, at], localT[:, at], bank[6 + half][:, 0:STEPS // 2], ALU.add)
                dve.tensor_copy(stepI[:, 1, at], bank[6 + half][:, 0:STEPS // 2])
            link(dve.scalar_tensor_tensor(own[:, :], localT[:, :], 0.0, wT[:, :], ALU.is_ge, ALU.mult))
            link(dve.tensor_scalar(stepI[:, 1, :], stepI[:, 1, :], DIGIT, None, ALU.logical_shift_right))
            dve.scalar_tensor_tensor(own[:, :], localT[:, :], float(P), own[:, :], ALU.is_lt, ALU.mult)
            dve.tensor_scalar(stripI[:, 0, :], stepI[:, 0, :], STRIP - 1, None, ALU.bitwise_and)
            dve.tensor_tensor(ring1[:, 0:STEPS].rearrange("p (b g t) -> p b g t", g=16, t=PACK),
                              stepI[:, 1, :].rearrange("p (b g t) -> p b g t", g=16, t=PACK),
                              sameGroup[:, :, :].unsqueeze(1).to_broadcast([P, BATCHES, 16, PACK]), ALU.mult)
            link(dve.tensor_scalar(stripI[:, 1, :], stepI[:, 0, :], 5, None, ALU.arith_shift_right))
            dve.scalar_tensor_tensor(strip[:, :], stepI[:, 1, :], -float(PACK), stripI[:, 1, :],
                                     ALU.mult, ALU.add)
            link(dve.tensor_reduce(target[:, :, :], ring1[:, 0:STEPS].rearrange(
                "p (b g t) -> p b t g", g=16, t=PACK), AX.X, ALU.add))
            link(dve.tensor_scalar(target[:, :, :], target[:, :, :], offset[:, 0:1], None, ALU.add))

            def steps_of(a, i, j, wide):
                return a[:, ds(i * (2 * BATCH) + j * BATCH, BATCH)].unsqueeze(2).to_broadcast([P, BATCH, wide])

            def matched(i, j):
                at = stripHot(j).rearrange("p (s r) -> p s r", r=STRIPS)
                dve.tensor_tensor(at, iota[:, 0:STRIPS].unsqueeze(1).to_broadcast([P, BATCH, STRIPS]),
                                  steps_of(strip, i, j, STRIPS), ALU.is_equal).then_inc(s_matched, 1)
                dve.tensor_tensor(placeHot(j).rearrange("p (s r) -> p s r", r=STRIP),
                                  iota[:, 0:STRIP].unsqueeze(1).to_broadcast([P, BATCH, STRIP]),
                                  steps_of(stripI[:, 0, :], i, j, STRIP), ALU.is_equal)
                dve.wait_ge(s_matched, i * 2 + (j + 1))
                dve.tensor_tensor(at, at, steps_of(own, i, j, STRIPS), ALU.mult).then_inc(s_batch, 1)

            def cut(i, j):
                dve.wait_ge(s_crossed, i * 2 + (j + 1))
                dve.tensor_tensor(masked(j).rearrange("p (g s) -> p g s", g=16),
                                  bank[j][:, :].rearrange("p (g s) -> p g s", g=16),
                                  sameStep[:, :, :].rearrange("p t r -> p (t r)").unsqueeze(1).to_broadcast(
                                      [P, 16, PACK * STRIPS]), ALU.mult).then_inc(s_masked, 1)
                dve.wait_ge(s_masked, i * 2 + (j + 1))
                dve.tensor_reduce(sumsOf(j).rearrange("p (g r) -> p g r", r=STRIPS), masked(j).rearrange(
                    "p (g t r) -> p g r t", g=16, t=PACK), AX.X, ALU.add).then_inc(s_cut, 1)

            def ready(i, j):
                dve.wait_ge(s_swapped, i * 2 + (j + 1))
                for t in range(PACK):
                    dve.tensor_scalar(targetHot(j, t), columns[:, :], target[:, ds(i * 2 + j, 1), t],
                                      None, ALU.is_equal)
                dve.tensor_copy(swappedOf(j), bank[2 + j][:, 0:P]).then_inc(s_ready, 1)

            sweep(dve, BATCHES, [(0, matched), (1, cut), (2, ready)], block=2)
            dve.wait_ge(s_strips, 1)
            dve.tensor_copy(strips[:, :], bank[4][0:STRIP, 0:PLACES]).then_inc(s_stacked, 1)
            dve.wait_ge(s_total, 1)
            degree = bank[5][:, 0:WINDOWS]
            link(dve.tensor_scalar(deg[:, 0, :], degree, 0.0, None, ALU.is_gt))
            link(dve.tensor_tensor(deg[:, 1, :], degree, deg[:, 0, :], ALU.mult))
            link(dve.scalar_tensor_tensor(deg[:, 1, :], deg[:, 1, :], 1.0, deg[:, 0, :], ALU.add, ALU.subtract))
            dve.drain().then_inc(s_var, 1)
            dve.wait_ge(s_root, 2)
            link(dve.reciprocal(dis[:, :], spread[:, :]))
            link(dve.tensor_tensor(dis[:, :], dis[:, :], deg[:, 0, :], ALU.mult))

            dve.wait_ge(s_h, WINDOWS)
            for g in range(GROUPS):
                ws = slice(g * GROUP, (g + 1) * GROUP)
                dve.tensor_tensor(T[:, ws, :], Hn[:, ws, :],
                                  dis[:, ws].unsqueeze(2).to_broadcast([P, GROUP, H]),
                                  ALU.mult).then_inc(s_scaled, 1)
            link(dve.tensor_tensor(X[:, :, :], X[:, :, :], Hn[:, :, :], ALU.add))
            link(dve.memset(S[:, :], 0.0))
            extras = dve.value_load(flags[0:1, 1:2])

            def sums(layer, lane_no):
                lane, first, count = LANES[lane_no]

                def build(i, j):
                    dve.wait_ge(lane.done, i * BLOCK + (layer * count + j + DONE0 - BLOCK + 1))
                    at = ds(i * BLOCK + (first + j), 1)
                    if layer < 2:
                        dve.tensor_scalar(hot[:, j, :], iota[:, :], localT[:, at], wT[:, at],
                                          ALU.is_equal, ALU.mult).then_inc(lane.hot, 1)
                    else:
                        dve.tensor_scalar(hot[:, j, :], iota[:, :], localT[:, at], None,
                                          ALU.is_equal).then_inc(lane.hot, 1)

                def scored(i, j):
                    dve.wait_ge(lane.z, i * BLOCK + (j + 1))
                    dve.scalar_tensor_tensor(junk[:, j % 2, :], bank[6 + j % 2][:, 0:H], 0.0, vec[:, 3, :],
                                             ALU.max, ALU.mult, accum_out=score[:, j % RING:j % RING + 1]
                                             ).then_inc(lane.scored, 1)

                bases = []

                def load_bases(i, j):
                    if j % BASES == 0:
                        bases[:] = nc.values_load_multi_w_load_instructions(
                            baseT[0:1, ds(i * BLOCK + (first + j), BASES)], engines=[mybir.EngineType.DVE],
                            min_val=0, max_val=SUMS - P)[1]

                def added(i, j):
                    dve.wait_ge(lane.done, i * BLOCK + (layer * count + j + DONE0 + 1))
                    dve.wait_ge(lane.added, i * BLOCK + (layer * count + j + ADDED0))
                    at = ds(bases[j % BASES], P)
                    dve.tensor_tensor(S[:, at], S[:, at], bank[j % 4][:, 0:P], ALU.add).then_inc(lane.added, 1)

                sweep(dve, count, [(0, build)] + [(SCORE_LAG, scored)] * (layer == 2)
                      + [(ADD_LAG, load_bases), (ADD_LAG, added)])

            for layer in range(3):
                if layer == 2:
                    dve.wait_ge(s_tables, 16 * (3 * GROUPS + 1))
                    link(dve.memset(S[:, :], 0.0))
                    for g in range(GROUPS):
                        ws = slice(g * GROUP, (g + 1) * GROUP)
                        dve.tensor_tensor(X[:, ws, :], X[:, ws, :],
                                          vec[:, 5, :].unsqueeze(1).to_broadcast([P, GROUP, H]), ALU.add)
                sums(layer, 0)
                with dve.If(extras > 0):
                    dve.wait_ge(main.added, ADDED0 + (layer + 1) * TILES)
                    sums(layer, 1)
                if layer < 2:
                    dve.wait_ge(s_weights, 16 * 10)
                    with dve.Fori(0, GROUPS) as g:
                        for k in range(GROUP):
                            w = g * GROUP + k
                            dve.wait_ge(s_product, g * GROUP + (layer * WINDOWS + k + 1))
                            dve.scalar_tensor_tensor(T[:, ds(w, 1), :], bank[k][:, 0:H], dis[:, ds(w, 1)],
                                                     vec[:, layer, :], ALU.mult, ALU.add).then_inc(s_applied, 1)
                if layer == 0:
                    link(dve.memset(S[:, :], 0.0))
                if layer == 1:
                    link(dve.drain())
                    with dve.Fori(0, WINDOWS) as w:
                        dve.scalar_tensor_tensor(X[:, ds(w, 1), :], T[:, ds(w, 1), :], 0.0, X[:, ds(w, 1), :],
                                                 ALU.max, ALU.add)
                    link(dve.drain())
                    statistics(X)
                    scales(3, 2)
                    with dve.Fori(0, GROUPS) as g:
                        for k in range(GROUP):
                            w = g * GROUP + k
                            dve.wait_ge(s_ab, g * GROUP + (k + 1))
                            ab = bank[ab_bank(k)]
                            dve.tensor_tensor(T[:, ds(w, 1), :], ab[:, 0:H], vec[:, 2, :], ALU.add)
                            dve.tensor_copy(S[:, ds(w * H, H)], ab[:, H:2 * H]).then_inc(s_abread, 1)

            with dve.Fori(0, GROUPS) as g:
                for k in range(GROUP):
                    w = g * GROUP + k
                    dve.wait_ge(s_back, g * GROUP + (k + 1))
                    dve.tensor_tensor(Hn[:, ds(w, 1), :], bank[k][:, 0:P], Hn[:, ds(w, 1), :],
                                      ALU.add).then_inc(s_attended, 1)
            link(dve.drain())
            statistics(Hn)
            scales(4, 3)
            for g in range(GROUPS):
                ws = slice(g * GROUP, (g + 1) * GROUP)
                dve.wait_ge(s_normed, (g + 1) * GROUP)
                link(dve.tensor_tensor(T[:, ws, :], T[:, ws, :],
                                       vec[:, 4, :].unsqueeze(1).to_broadcast([P, GROUP, H]), ALU.mult))
                dve.tensor_tensor(T[:, ws, :], T[:, ws, :], X[:, ws, :], ALU.add).then_inc(s_final, 1)


_INS = ["x", "src", "dst", "edge_weight", "L0_gnn_W1", "L0_gnn_b1", "L0_gnn_W2", "L0_gnn_b2", "L1_gnn_W1",
        "L1_gnn_b1", "L1_gnn_W2", "L1_gnn_b2", "L1_gnn_gamma", "L1_gnn_beta"]


def kernel(**inputs):
    import numpy as np
    import concourse.bacc as bacc
    from concourse import mybir
    from concourse.bass_utils import run_bass_kernel_spmd as run

    nc = bacc.Bacc("TRN2", target_bir_lowering=False, num_devices=1)
    arrays, args = {}, []
    for name in _INS:
        a = np.ascontiguousarray(inputs[name])
        arrays[f"in_{name}"] = a
        args.append(nc.dram_tensor(f"in_{name}", a.shape, mybir.dt.from_np(a.dtype), kind="ExternalInput").ap())
    f32 = mybir.dt.float32
    args.append(nc.dram_tensor("out", (N, H), f32, kind="ExternalOutput").ap())
    for name, shape in (("rows1", (WINDOWS * P, H)), ("rows2", (WINDOWS * P, H)),
                        ("rows3", (WINDOWS * P, 2 * H)), ("brows", (SUMS, H))):
        args.append(nc.dram_tensor(name, shape, f32, kind="Internal").ap())
    args.append(nc.dram_tensor("records", (TILES * P, RECORD), mybir.dt.int32, kind="Internal").ap())
    gnn_kernel(nc, *args)
    r = run(nc, [arrays], core_ids=[0])
    return r.results[0]["out"]
```

```python
import concourse.bass as bass
from concourse import mybir
from contextlib import ExitStack


P = 128
N, H, E = 6250, 128, 100000
WINDOWS = -(-N // P)
LAST = N - (WINDOWS - 1) * P
BLOCK = 16
RING = 8
TILES = -(-E // (P * BLOCK)) * BLOCK
CHUNKS = 7
ROWS = TILES // CHUNKS
EXTRAS = -(-(N // P) // BLOCK) * BLOCK
STEPS = TILES + EXTRAS
SUMS = (N // P + 2) * P
GROUP = 7
GROUPS = WINDOWS // GROUP
EARLY = 5
FULL = E // (P * ROWS)
TAIL = E // P - FULL * ROWS
REST = E - (E // P) * P
NOWHERE = 16384.0
EPS = 1e-5
TURN_LAG, GATE_LAG, SCORE_LAG, OPEN_LAG, SUM_LAG, ADD_LAG = 1, 2, 3, 3, 6, 8
AT_ONCE = 4
BASES = 8
RECORD = 4
SORT = 4
DIGIT = 7
STRIP, STRIPS = 32, 8
PACK = P // STRIP
BATCH = 16 * PACK
BATCHES = STEPS // BATCH
PLACES = PACK * (WINDOWS + 1)


def gnn_kernel(nc, x, src, dst, weight, g_w1, g_b1, g_w2, g_b2,
               a_w1, a_b1, a_w2, a_b2, gamma, beta, out, rows1, rows2, rows3, brows, records):
    f32, i32 = mybir.dt.float32, mybir.dt.int32
    ALU, ACT, AX = mybir.AluOpType, mybir.ActivationFunctionType, mybir.AxisListType
    ds = bass.ds

    ctx = ExitStack()
    with ctx:
        def sb(name, shape, dt=f32):
            return ctx.enter_context(nc.sbuf_tensor(name, shape, dt))

        def sem(name):
            return ctx.enter_context(nc.semaphore(name))

        bank = [ctx.enter_context(nc.psum_tensor(f"bank{i}", [P, 512], f32)) for i in range(8)]

        srcR = sb("srcR", [ROWS, CHUNKS, P], i32)
        dstR = sb("dstR", [ROWS, CHUNKS, P], i32)
        wR = sb("wR", [ROWS, CHUNKS, P])
        nextR = sb("nextR", [ROWS, CHUNKS, P], i32)
        srcF = sb("srcF", [ROWS, CHUNKS, P])
        dstF = sb("dstF", [ROWS, CHUNKS, P])
        localF = sb("localF", [ROWS, CHUNKS, P])
        cols = sb("cols", [ROWS, 9, CHUNKS])
        (VIOLATIONS,
         COUNT,
         TOTAL,
         THROUGH,
         UPTO,
         BEFORE,
         ORIGIN,
         SHIFT) = range(8)
        spanI = sb("spanI", [ROWS, 2, CHUNKS], i32)
        chosen = sb("chosen", [ROWS, CHUNKS, EXTRAS])
        srcT = sb("srcT", [P, STEPS], i32)
        localT = sb("localT", [P, STEPS])
        wT = sb("wT", [P, STEPS])
        baseT = sb("baseT", [1, STEPS], i32)
        baseF = sb("baseF", [1, STEPS])
        digitI = sb("digitI", [P, TILES], i32)
        digits = sb("digits", [P, TILES])
        flags = sb("flags", [1, 2], i32)

        iota = sb("iota", [P, P])
        ident = sb("ident", [P, P])
        upper = sb("upper", [P, P])
        ones = sb("ones", [P, P])
        zeros = sb("zeros", [P, P])
        W1 = sb("W1", [P, H])
        W2 = sb("W2", [P, H])
        AW = sb("AW", [P, 2, H])
        vec = sb("vec", [P, 6, H])
        ab2 = sb("ab2", [P, 1])

        X = sb("X", [P, WINDOWS, H])
        Hn = sb("Hn", [P, WINDOWS, H])
        T = sb("T", [P, WINDOWS, H])
        S = sb("S", [P, SUMS])
        stats = sb("stats", [P, WINDOWS, 6])
        mean = sb("mean", [P, WINDOWS])
        var = sb("var", [P, WINDOWS])
        rstd = sb("rstd", [P, WINDOWS])
        shift = sb("shift", [P, WINDOWS])
        deg = sb("deg", [P, 2, WINDOWS])
        spread = sb("spread", [P, WINDOWS])
        eps = sb("eps", [P, 1])
        dis = sb("dis", [P, WINDOWS])

        recF = T[:, 0:WINDOWS // 2 + 1, :].rearrange("p w f -> p (w f)")[:, 0:TILES * RECORD].rearrange(
            "p (t r) -> p t r", r=RECORD)
        recI = recF.bitcast(i32)
        strict = sb("strict", [P, P])
        moved = sb("moved", [P, SORT, RECORD], i32)
        place = sb("place", [P, SORT], i32)
        placeF = sb("placeF", [P, 1])
        counts = sb("counts", [P, 1])
        start = sb("start", [1, P])
        reached = sb("reached", [1, P])

        byStep = S[:, 0:6 * STEPS].rearrange("p (a s) -> p a s", s=STEPS)
        stepI = byStep[:, 0:2, :].bitcast(i32)
        stripI = byStep[:, 2:4, :].bitcast(i32)
        strip = byStep[:, 4, :]
        own = byStep[:, 5, :]
        target = sb("target", [P, BATCHES, PACK])
        offset = sb("offset", [P, 1])
        rowI = sb("rowI", [P, 3], i32)
        columns = sb("columns", [P, PLACES])
        sameStep = sb("sameStep", [P, PACK, STRIPS])
        sameGroup = sb("sameGroup", [P, 16, PACK])
        stack = sb("stack", [STRIP, PACK, P])
        strips = sb("strips", [STRIP, PLACES])

        picked = sb("picked", [P, 2, RING], i32)
        msg = sb("msg", [P, BLOCK, 2 * H])
        hot = sb("hot", [P, BLOCK, P])
        hotT = sb("hotT", [P, 4, P])
        gated = sb("gated", [P, 4, P])
        bwin = sb("bwin", [P, BLOCK, H])
        junk = sb("junk", [P, 2, P])
        score = sb("score", [P, RING])
        gate = sb("gate", [P, RING])

        ring1 = msg[:, :, :].rearrange("p s f -> p (s f)")
        ring2 = hot[:, :, :].rearrange("p s f -> p (s f)")
        ring3 = bwin[:, :, :].rearrange("p s f -> p (s f)")

        def placeHot(j):
            return ring1[:, j * BATCH * STRIP:(j + 1) * BATCH * STRIP]

        def stripHot(j):
            return ring2[:, j * BATCH * STRIPS:(j + 1) * BATCH * STRIPS]

        def masked(j):
            return ring2[:, (2 + j) * BATCH * STRIPS:(3 + j) * BATCH * STRIPS]

        def targetHot(j, t):
            return ring3[:, (j * PACK + t) * PLACES:(j * PACK + t + 1) * PLACES]

        def sumsOf(j):
            return gated[:, j, :]

        def swappedOf(j):
            return hotT[:, j, :]

        s_const = sem("s_const")
        s_in = sem("s_in")
        s_pad = sem("s_pad")
        s_weights = sem("s_weights")
        s_x = sem("s_x")
        s_xpad = sem("s_xpad")
        s_dve = sem("s_dve")
        s_pre = sem("s_pre")
        s_prep = sem("s_prep")
        s_flag = sem("s_flag")
        s_sclear = sem("s_sclear")
        s_sload = sem("s_sload")
        s_shot = sem("s_shot")
        s_scount = sem("s_scount")
        s_stotal = sem("s_stotal")
        s_scounts = sem("s_scounts")
        s_sstart = sem("s_sstart")
        s_sstarted = sem("s_sstarted")
        s_smark = sem("s_smark")
        s_srank = sem("s_srank")
        s_splace = sem("s_splace")
        s_swrite = [sem(f"s_swrite{j}") for j in range(SORT)]
        s_sfree = sem("s_sfree")
        s_srows = sem("s_srows")
        s_steps = sem("s_steps")
        s_matched = sem("s_matched")
        s_batch = sem("s_batch")
        s_crossed = sem("s_crossed")
        s_masked = sem("s_masked")
        s_cut = sem("s_cut")
        s_swapped = sem("s_swapped")
        s_taken = sem("s_taken")
        s_ready = sem("s_ready")
        s_strips = sem("s_strips")
        s_stacked = sem("s_stacked")
        s_total = sem("s_total")
        s_var = sem("s_var")
        s_root = sem("s_root")
        s_scale = sem("s_scale")
        s_h = sem("s_h")
        s_scaled = sem("s_scaled")
        s_zeroed = sem("s_zeroed")
        s_product = sem("s_product")
        s_applied = sem("s_applied")
        s_rows = sem("s_rows")
        s_table = sem("s_table")
        s_flip = sem("s_flip")
        s_flipped = sem("s_flipped")
        s_a = sem("s_a")
        s_b = sem("s_b")
        s_aread = sem("s_aread")
        s_bread = sem("s_bread")
        s_streamed = sem("s_streamed")
        s_tables = sem("s_tables")
        s_stored = [sem(f"s_stored{n}") for n in range(2)]
        s_back = sem("s_back")
        s_attended = sem("s_attended")
        s_normed = sem("s_normed")
        s_final = sem("s_final")
        s_issue = sem("s_issue")
        s_out = sem("s_out")

        class Lane:
            def __init__(self, tag):
                self.listed = [sem(f"listed{i}{tag}") for i in range(2)]
                self.gathered = [sem(f"gathered{i}{tag}") for i in range(BLOCK)]
                self.loaded = [sem(f"loaded{i}{tag}") for i in range(BLOCK)]
                self.hot = sem(f"hot{tag}")
                self.done = sem(f"done{tag}")
                self.added = sem(f"added{tag}")
                self.turned = sem(f"turned{tag}")
                self.hotT = sem(f"hotT{tag}")
                self.z = sem(f"z{tag}")
                self.scored = sem(f"scored{tag}")
                self.opened = sem(f"opened{tag}")
                self.gated = sem(f"gated{tag}")

        main, extra = Lane(""), Lane("x")
        LANES = ((main, 0, TILES), (extra, TILES, EXTRAS))
        DONE0, ADDED0, HOTT0, SCORED0 = 16, 8, 2, 2

        def sweep(engine, steps, stages, block=BLOCK):
            def place(i, j):
                for lag, do in stages:
                    before = (lag - j + block - 1) // block if lag > j else 0
                    if not isinstance(i, int) or 0 <= i * block + j - lag < steps:
                        do(i - before if before else i, j - lag + before * block)

            for j in range(block):
                place(0, j)
            with engine.Fori(1, steps // block) as i:
                for j in range(block):
                    place(i, j)
            for n in range(steps // block * block, steps + max(lag for lag, _ in stages)):
                place(n // block, n % block)

        def of_group(g):
            return range(g * GROUP, (g + 1) * GROUP)

        def span(g):
            return slice(g * GROUP, (g + 1) * GROUP)

        PRODUCT, FLIP, A_BANK, B_BANK = 0, 2, 4, 6

        block = ctx.enter_context(nc.Block())

        @block.sync
        def _(sp):
            def rows_of(a, first, rest):
                whole = first + FULL * ROWS * P
                tail = whole + TAIL * P
                return (a[first:whole].rearrange("(k q j) -> q k j", q=ROWS, j=P),
                        a[whole:tail].rearrange("(q j) -> q j", j=P),
                        a[tail:tail + rest].rearrange("(q j) -> q j", q=1))

            sp.wait_ge(s_pad, 1)
            for dest, a, first, rest in ((dstR, dst, 0, REST), (nextR, dst, 1, REST - 1),
                                         (srcR, src, 0, REST), (wR, weight, 0, REST)):
                whole, tail, last = rows_of(a, first, rest)
                sp.dma_start(dest[:, 0:FULL, :], whole).then_inc(s_in, 16)
                sp.dma_start(dest[0:TAIL, FULL, :], tail).then_inc(s_in, 16)
                sp.dma_start(dest[TAIL:TAIL + 1, FULL, 0:rest], last).then_inc(s_in, 16)
            sp.dma_start(X[:, 0:WINDOWS - 1, :],
                         x[0:(WINDOWS - 1) * P, :].rearrange("(w p) f -> p w f", p=P)).then_inc(s_x, 16)
            sp.wait_ge(s_xpad, 1)
            sp.dma_start(X[0:LAST, WINDOWS - 1, :], x[(WINDOWS - 1) * P:N, :]).then_inc(s_x, 16)
            sp.dma_start(W1[:, :], g_w1).then_inc(s_weights, 16)
            sp.dma_start(W2[:, :], g_w2).then_inc(s_weights, 16)
            sp.dma_start(AW[:, :, :], a_w1.rearrange("(k p) f -> p k f", p=P)).then_inc(s_weights, 16)
            for n, v in enumerate((g_b1, g_b2, a_b1, a_w2.rearrange("f o -> (f o)"), gamma, beta)):
                sp.dma_start(vec[:, n, :], v.unsqueeze(0).to_broadcast([P, H])).then_inc(s_weights, 16)
            sp.dma_start(ab2[:, :], a_b2.unsqueeze(0).to_broadcast([P, 1])).then_inc(s_weights, 16)

            def nodes(table, g, cols=slice(0, H)):
                return table[g * GROUP * P:(g + 1) * GROUP * P, cols].rearrange("(w p) f -> p w f", p=P)

            def group(a, g):
                return a[:, g * GROUP:(g + 1) * GROUP, :]

            sp.wait_ge(s_flag, 1)
            disorder = sp.value_load(flags[0:1, 0:1])
            with sp.If(disorder > 0), nc.allow_non_contiguous_dma(reason="edges out of order only"):
                sp.wait_ge(s_sclear, 1)
                whole = E // P * P
                for n, (a, rec) in enumerate(((src, recI), (dst, recI), (weight, recF))):
                    sp.dma_start(rec[:, 0:E // P, n], a[0:whole].rearrange("(t p) -> p t", p=P)
                                 ).then_inc(s_sload, 16)
                    sp.dma_start(rec[0:REST, E // P, n:n + 1], a[whole:E].rearrange("(p t) -> p t", t=1)
                                 ).then_inc(s_sload, 16)
                for j in range(SORT):
                    sp.wait_ge(s_swrite[j], 16 * (TILES // SORT))
                sp.dma_start(recI[:, :, :], records.rearrange("(t p) r -> p t r", p=P)).then_inc(s_sload, 16)
                for j in range(SORT):
                    sp.wait_ge(s_swrite[j], 2 * 16 * (TILES // SORT))
                for n, rows in enumerate((srcR, dstR, wR[:, :, :].bitcast(i32))):
                    for k in range(CHUNKS):
                        sp.dma_start(rows[:, k, :], records[k * ROWS * P:(k + 1) * ROWS * P, n].rearrange(
                            "(q j) -> q j", j=P)).then_inc(s_srows, 16)
            sp.wait_ge(s_steps, 1)
            extras = sp.value_load(flags[0:1, 1:2])

            def edges(layer, lane_no):
                lane, first, count = LANES[lane_no]
                blocks = count // BLOCK

                def indices(i, j):
                    if j % RING:
                        return
                    half = j // RING
                    if not (isinstance(i, int) and i + layer == 0):
                        for slot in range(half * RING, (half + 1) * RING):
                            sp.wait_ge(lane.gathered[slot], i * 16 + 16 * layer * blocks)
                    sp.dma_start(picked[:, half, :], srcT[:, ds(i * BLOCK + (first + j), RING)]
                                 ).then_inc(lane.listed[half], 16)

                bases = []

                def rows(i, j):
                    if j == 0:
                        bases[:] = nc.values_load_multi_w_load_instructions(
                            baseT[0:1, ds(i * BLOCK + first, BLOCK)], engines=[mybir.EngineType.SP],
                            min_val=0, max_val=SUMS - P)[1]
                    base = bases[j]
                    sp.wait_ge(lane.done, i * BLOCK + (layer * count + j + DONE0 - BLOCK + 1))
                    sp.dma_start(bwin[:, j, :], brows[ds(base, P), :]).then_inc(lane.loaded[j], 16)

                sweep(sp, count, [(0, indices)] + [(0, rows)] * (layer == 2))

            for layer in range(3):
                if layer == 0:
                    for g in range(GROUPS):
                        sp.wait_ge(s_scaled, g + 1)
                        sp.dma_start(nodes(rows1, g), group(T, g)).then_inc(s_table, 16)
                elif layer == 1:
                    for g in range(GROUPS):
                        sp.wait_ge(s_rows, (g + 1) * GROUP)
                        sp.dma_start(nodes(rows2, g), group(T, g)).then_inc(s_table, 16)
                else:
                    for g in range(GROUPS):
                        sp.wait_ge(s_aread, (g + 1) * GROUP)
                        sp.wait_ge(s_bread, (g + 1) * GROUP)
                        sp.dma_start(nodes(rows3, g), group(Hn, g)).then_inc(s_tables, 16)
                        sp.dma_start(nodes(rows3, g, slice(H, 2 * H)), group(T, g)).then_inc(s_tables, 16)
                        sp.dma_start(nodes(brows, g), S[:, g * GROUP * P:(g + 1) * GROUP * P].rearrange(
                            "p (w f) -> p w f", f=H)).then_inc(s_stored[g >= EARLY], 16)
                    sp.dma_start(brows[WINDOWS * P:SUMS, :], zeros[:, :]).then_inc(s_stored[1], 16)
                    sp.wait_ge(s_stored[0], 16 * EARLY)
                    sp.wait_ge(s_stored[1], 16 * (GROUPS - EARLY + 1))
                edges(layer, 0)
                with sp.If(extras > 0):
                    sp.wait_ge(main.done, DONE0 + (layer + 1) * TILES)
                    edges(layer, 1)

            for g in range(GROUPS):
                sp.wait_ge(s_final, g + 1)
                full = GROUP if g < GROUPS - 1 else GROUP - 1
                w0 = g * GROUP
                sp.dma_start(out[w0 * P:(w0 + full) * P, :].rearrange("(w p) f -> p w f", p=P),
                             T[:, w0:w0 + full, :]).then_inc(s_out, 16)
            sp.dma_start(out[(WINDOWS - 1) * P:N, :], T[0:LAST, WINDOWS - 1, :]).then_inc(s_out, 16)
            sp.wait_ge(s_out, 16 * (GROUPS + 1))

        @block.gpsimd
        def _(pool):
            pool.memset(ones[:, :], 1.0).then_inc(s_const, 1)
            pool.memset(zeros[:, :], 0.0).then_inc(s_const, 1)
            pool.iota(iota[:, :], [[1, P]], base=0, channel_multiplier=0,
                      allow_small_or_imprecise_dtypes=True).then_inc(s_const, 1)
            pool.wait_ge(s_const, 3)
            pool.affine_select(out=ident[:, :], in_=ones[:, :], pattern=[[1, P]], compare_op=ALU.is_equal,
                               fill=0.0, base=0, channel_multiplier=-1).then_inc(s_const, 1)
            pool.affine_select(out=strict[:, :], in_=ones[:, :], pattern=[[1, P]], compare_op=ALU.is_gt,
                               fill=0.0, base=0, channel_multiplier=-1).then_inc(s_const, 1)
            pool.affine_select(out=upper[:, :], in_=ones[:, :], pattern=[[1, P]], compare_op=ALU.is_ge,
                               fill=0.0, base=0, channel_multiplier=-1).then_inc(s_const, 1)
            pool.iota(columns[:, :], [[1, PLACES]], base=0, channel_multiplier=0,
                      allow_small_or_imprecise_dtypes=True).then_inc(s_const, 1)
            pool.iota(rowI[:, 0:1], [[0, 1]], base=0, channel_multiplier=1).then_inc(s_const, 1)
            for kept, size, inner in ((sameStep, STRIP, STRIPS), (sameGroup, STRIPS, PACK)):
                count = P // size
                pool.affine_select(out=kept[:, :, :], in_=ones[:, 0:count * inner].rearrange(
                    "p (a b) -> p a b", b=inner), pattern=[[-size, count], [0, inner]], compare_op=ALU.is_ge,
                    fill=0.0, base=0, channel_multiplier=1).then_inc(s_const, 1)
            pool.wait_ge(s_const, 10)
            for kept, size, inner in ((sameStep, STRIP, STRIPS), (sameGroup, STRIPS, PACK)):
                pool.affine_select(out=kept[:, :, :], in_=kept[:, :, :],
                                   pattern=[[size, P // size], [0, inner]], compare_op=ALU.is_ge,
                                   fill=0.0, base=size - 1, channel_multiplier=-1).then_inc(s_const, 1)
            for q in range(PACK):
                pool.affine_select(out=stack[:, q, :], in_=ones[0:STRIP, :], pattern=[[1, P]],
                                   compare_op=ALU.is_equal, fill=0.0, base=-STRIP * q,
                                   channel_multiplier=-1).then_inc(s_const, 1)
            pool.wait_ge(s_flag, 1)
            disorder = pool.value_load(flags[0:1, 0:1])
            with pool.If(disorder > 0):
                for digit in range(2):
                    if digit == 1:
                        pool.wait_ge(s_sload, 16 * 7)
                    with pool.Fori(0, TILES // SORT) as i:
                        for j in range(SORT):
                            pool.wait_ge(s_splace, i * SORT + (digit * TILES + j + 1))
                            pool.sem_inc(s_issue, 1)
                            pool.indirect_dma_start(
                                out=records[:, :], out_offset=bass.IndirectOffsetOnAxis(ap=place[:, j:j + 1], axis=0),
                                in_=moved[:, j, :], in_offset=None).then_inc(s_swrite[j], 16)
                        for j in range(SORT):
                            pool.wait_ge(s_swrite[j], i * 16 + 16 * (digit * (TILES // SORT) + 1))
                        pool.sem_inc(s_sfree, SORT)
            pool.wait_ge(s_h, WINDOWS)
            pool.tensor_tensor(X[:, :, :], X[:, :, :], Hn[:, :, :], ALU.add).then_inc(s_streamed, 1)
            pool.wait_ge(s_total, 1)
            pool.memset(S[:, :], 0.0).then_inc(s_zeroed, 1)
            pool.wait_ge(s_steps, 1)
            extras = pool.value_load(flags[0:1, 1:2])

            def gathers(layer, lane_no):
                lane, first, count = LANES[lane_no]
                table, width = ((rows1, H), (rows2, H), (rows3, 2 * H))[layer]
                def gather(i, j):
                    half = j // RING
                    if j % RING == 0:
                        pool.wait_ge(lane.listed[half], i * 16 + 16 * (layer * (count // BLOCK) + 1))
                    if j % 4 == 0:
                        pool.wait_ge(lane.done, i * BLOCK + (layer * count + j + 3 + DONE0 - BLOCK + 1))
                        pool.sem_inc(s_issue, 1)
                    pool.indirect_dma_start(
                        out=msg[:, j, 0:width], out_offset=None, in_=table[:, :],
                        in_offset=bass.IndirectOffsetOnAxis(ap=picked[:, half, j % RING:j % RING + 1], axis=0),
                    ).then_inc(lane.gathered[j], 16)

                with pool.Fori(0, count // BLOCK) as i:
                    for j in range(BLOCK):
                        gather(i, j)

            for layer in range(3):
                if layer < 2:
                    pool.wait_ge(s_table, 16 * GROUPS * (layer + 1))
                else:
                    for g in range(GROUPS):
                        pool.wait_ge(s_h, WINDOWS + (g + 1) * GROUP)
                        pool.tensor_tensor(X[:, span(g), :], X[:, span(g), :],
                                           vec[:, 5, :].unsqueeze(1).to_broadcast([P, GROUP, H]),
                                           ALU.add).then_inc(s_streamed, 1)
                    pool.wait_ge(s_tables, 16 * 2 * GROUPS)
                gathers(layer, 0)
                with pool.If(extras > 0):
                    pool.wait_ge(main.done, DONE0 + (layer + 1) * TILES)
                    gathers(layer, 1)

            pool.wait_ge(s_streamed, 1 + GROUPS)
            for g in range(GROUPS):
                pool.wait_ge(s_normed, (g + 1) * GROUP)
                pool.tensor_tensor(T[:, span(g), :], T[:, span(g), :],
                                   vec[:, 4, :].unsqueeze(1).to_broadcast([P, GROUP, H]),
                                   ALU.mult).then_inc(s_scaled, 1)
                pool.wait_ge(s_scaled, GROUPS + g + 1)
                pool.tensor_tensor(T[:, span(g), :], T[:, span(g), :], X[:, span(g), :],
                                   ALU.add).then_inc(s_final, 1)

        @block.tensor
        def _(pe):
            pe.sem_inc(main.done, DONE0)
            pe.sem_inc(extra.done, DONE0)
            pe.wait_ge(s_const, 6)
            pe.wait_ge(s_pre, 1)
            pe.matmul(bank[0][:, 0:1], ones[0:ROWS, :], cols[0:ROWS, VIOLATIONS, 0:1],
                      start=True, stop=True).then_inc(s_prep, 1)

            pe.wait_ge(s_flag, 1)
            disorder = pe.value_load(flags[0:1, 0:1])
            with pe.If(disorder > 0):
                pe.sem_inc(s_scount, SORT)
                for digit in range(2):
                    pe.matmul(bank[0][:, 0:1], zeros[:, :], zeros[:, 0:1], start=True, stop=False,
                              skip_group_check=True)
                    with pe.Fori(0, TILES // SORT) as i:
                        for j in range(SORT):
                            pe.wait_ge(s_shot, i * SORT + (digit * TILES + j + 1))
                            pe.matmul(bank[0][:, 0:1], hot[:, j, :], ones[:, 0:1], start=False, stop=False,
                                      skip_group_check=True).then_inc(s_scount, 1)
                    pe.matmul(bank[0][:, 0:1], zeros[:, :], zeros[:, 0:1], start=False, stop=True,
                              skip_group_check=True).then_inc(s_stotal, 1)
                    pe.wait_ge(s_scounts, digit + 1)
                    pe.matmul(bank[1][0:1, 0:P], counts[:, :], strict[:, :], start=True, stop=True
                              ).then_inc(s_sstart, 1)
                    pe.wait_ge(s_sstarted, digit + 1)
                    pe.matmul(bank[3][0:1, 0:P], ones[0:1, 0:1], start[:, :], start=True, stop=False,
                              skip_group_check=True)
                    with pe.Fori(0, TILES // SORT) as i:
                        for j in range(SORT):
                            pe.wait_ge(s_smark, i * SORT + (digit * TILES + j + 1))
                            pe.matmul(bank[2][:, 0:P], strict[:, :], hot[:, 8 + j, :], start=True, stop=False)
                            pe.matmul(bank[2][:, 0:P], ones[0:1, :], reached[:, :], start=False, stop=True)
                            pe.matmul(bank[3][0:1, 0:P], ones[:, 0:1], hot[:, 8 + j, :], start=False, stop=False,
                                      skip_group_check=True).then_inc(s_srank, 1)
                    pe.wait_ge(s_splace, (digit + 1) * TILES)
                    pe.matmul(bank[3][0:1, 0:P], zeros[:, 0:1], zeros[:, :], start=False, stop=True,
                              skip_group_check=True)

            pe.wait_ge(s_pre, 2)
            pe.matmul(bank[1][0:ROWS, 0:CHUNKS], upper[0:ROWS, 0:ROWS], cols[0:ROWS, COUNT, :],
                      start=True, stop=True).then_inc(s_prep, 1)
            pe.matmul(bank[2][:, 0:CHUNKS], ones[0:ROWS, :], cols[0:ROWS, COUNT, :],
                      start=True, stop=True).then_inc(s_prep, 1)
            pe.wait_ge(s_pre, 3)
            for a, rows in enumerate((srcF, localF, wR, dstF)):
                for k in range(CHUNKS):
                    last = pe.transpose(bank[2 * a + k // 4][:, (k % 4) * ROWS:(k % 4 + 1) * ROWS],
                                        rows[:, k, :], ident[0:ROWS, 0:ROWS])
                last.then_inc(s_prep, 1)
            pe.wait_ge(s_pre, 4)
            for a, rows in enumerate((srcF, localF, wR)):
                for k in range(CHUNKS):
                    last = pe.matmul(bank[a][:, 0:EXTRAS], rows[:, k, :], chosen[:, k, :],
                                     start=(k == 0), stop=(k == CHUNKS - 1))
                last.then_inc(s_prep, 1)
            for k in range(CHUNKS):
                last = pe.matmul(bank[3][0:1, 0:EXTRAS], cols[0:ROWS, ORIGIN, k:k + 1], chosen[:, k, :],
                                 start=(k == 0), stop=(k == CHUNKS - 1))
            last.then_inc(s_prep, 1)

            pe.wait_ge(s_pre, 5)
            for half in range(2):
                last = pe.matmul(bank[6 + half][:, 0:STEPS // 2], ones[0:1, :],
                                 baseF[:, half * (STEPS // 2):(half + 1) * (STEPS // 2)], start=True, stop=True)
            last.then_inc(s_prep, 1)

            def crossed(i, j):
                pe.wait_ge(s_batch, i * 2 + (j + 1))
                for g in range(16):
                    last = pe.matmul(bank[j][:, g * P // 4:(g + 1) * P // 4], placeHot(j)[:, g * P:(g + 1) * P],
                                     stripHot(j)[:, g * P // 4:(g + 1) * P // 4], start=True, stop=True)
                last.then_inc(s_crossed, 1)

            def swapped(i, j):
                pe.wait_ge(s_cut, i * 2 + (j + 1))
                pe.transpose(bank[2 + j][:, 0:P], sumsOf(j), ident[:, :]).then_inc(s_swapped, 1)

            def placed(i, j):
                pe.wait_ge(s_ready, i * 2 + (j + 1))
                for t in range(PACK):
                    pe.matmul(bank[4][0:STRIP, 0:PLACES], swappedOf(j)[:, t * STRIP:(t + 1) * STRIP],
                              targetHot(j, t), start=False, stop=False, skip_group_check=True)

            pe.wait_ge(s_const, 16)
            pe.matmul(bank[4][0:STRIP, 0:PLACES], zeros[:, 0:STRIP], columns[:, :], start=True, stop=False,
                      skip_group_check=True)
            sweep(pe, BATCHES, [(0, crossed), (1, swapped), (2, placed)], block=2)
            pe.matmul(bank[4][0:STRIP, 0:PLACES], zeros[:, 0:STRIP], columns[:, :], start=False, stop=True,
                      skip_group_check=True).then_inc(s_strips, 1)
            pe.wait_ge(s_stacked, 1)
            for q in range(PACK):
                last = pe.matmul(bank[5][:, 0:WINDOWS], stack[:, q, :],
                                 strips[:, q * (WINDOWS + 1):q * (WINDOWS + 1) + WINDOWS],
                                 start=(q == 0), stop=(q == PACK - 1))
            last.then_inc(s_total, 1)
            extras = pe.value_load(flags[0:1, 1:2])

            def products(layer, lane_no):
                lane, first, count = LANES[lane_no]
                blocks = count // BLOCK

                def rows_here(i, j):
                    pe.wait_ge(lane.gathered[j], i * 16 + 16 * (layer * blocks + 1))

                def bank_free(i, j):
                    pe.wait_ge(lane.added, i * BLOCK + (layer * count + j + ADDED0 - 4 + 1))

                def summed(i, j):
                    rows_here(i, j)
                    pe.wait_ge(lane.hot, i * BLOCK + (layer * count + j + 1))
                    bank_free(i, j)
                    pe.matmul(bank[j % 4][:, 0:P], msg[:, j, 0:H], hot[:, j, :],
                              start=True, stop=True).then_inc(lane.done, 1)

                def turn(i, j):
                    pe.wait_ge(lane.hot, i * BLOCK + (layer * count + j + 1))
                    pe.wait_ge(lane.hotT, i * BLOCK + (j + HOTT0 - 2 + 1))
                    pe.transpose(bank[4 + j % 2][:, 0:P], hot[:, j, :],
                                 ident[:, :]).then_inc(lane.turned, 1)

                def gate_input(i, j):
                    rows_here(i, j)
                    pe.wait_ge(lane.loaded[j], i * 16 + 16)
                    pe.wait_ge(lane.hotT, i * BLOCK + (j + HOTT0 + 1))
                    pe.wait_ge(lane.scored, i * BLOCK + (j + SCORED0 - 2 + 1))
                    pe.matmul(bank[6 + j % 2][:, 0:H], hotT[:, j % 4, :], bwin[:, j, :],
                              start=True, stop=False)
                    pe.matmul(bank[6 + j % 2][:, 0:H], ident[:, :], msg[:, j, H:2 * H],
                              start=False, stop=True).then_inc(lane.z, 1)

                def gated_sum(i, j):
                    pe.wait_ge(lane.gated, i * BLOCK + (j + 1))
                    bank_free(i, j)
                    pe.matmul(bank[j % 4][:, 0:P], msg[:, j, 0:H], gated[:, j % 4, :],
                              start=True, stop=True).then_inc(lane.done, 1)

                if layer < 2:
                    sweep(pe, count, [(0, summed)])
                else:
                    sweep(pe, count, [(TURN_LAG, turn), (GATE_LAG, gate_input), (SUM_LAG, gated_sum)])

            def product(layer, w, banks):
                n = layer * WINDOWS + w
                if layer or w >= banks:
                    pe.wait_ge(s_applied, max(n - banks, layer * WINDOWS - 1) + 1)
                pe.matmul(bank[w % banks][:, 0:H], S[:, w * P:(w + 1) * P], (W1, W2)[layer][:, :],
                          start=True, stop=True).then_inc(s_product, 1)

            for layer in range(3):
                if layer == 2:
                    pe.wait_ge(s_aread, WINDOWS)
                    pe.wait_ge(s_bread, WINDOWS)
                products(layer, 0)
                with pe.If(extras > 0):
                    pe.wait_ge(main.added, ADDED0 + (layer + 1) * TILES)
                    products(layer, 1)
                if layer < 2:
                    pe.wait_ge(s_weights, 16 * 10)
                    pe.wait_ge(main.added, ADDED0 + (layer + 1) * TILES)
                    with pe.If(extras > 0):
                        pe.wait_ge(extra.added, ADDED0 + (layer + 1) * EXTRAS)
                    if layer == 0:
                        for w in range(WINDOWS):
                            product(0, w, GROUP)
                if layer == 1:
                    for n in range(WINDOWS + 2 * GROUP + 1):
                        if n < WINDOWS:
                            product(1, n, 2)
                        w, u = n - 2 * GROUP, n - 2 * GROUP - 1
                        if 0 <= w < WINDOWS:
                            pe.wait_ge(s_h, WINDOWS + w + 1)
                            if w >= 2:
                                pe.wait_ge(s_flipped, w - 2 + 1)
                            pe.transpose(bank[FLIP + w % 2][:, 0:P], Hn[:, w, :],
                                         ident[:, :]).then_inc(s_flip, 1)
                        if u >= 0:
                            pe.wait_ge(s_flipped, u + 1)
                            for k, (first, done, read) in enumerate(((A_BANK, s_a, s_aread),
                                                                     (B_BANK, s_b, s_bread))):
                                if u >= 2:
                                    pe.wait_ge(read, u - 2 + 1)
                                pe.matmul(bank[first + u % 2][:, 0:H], hot[:, u % GROUP, :], AW[:, k, :],
                                          start=True, stop=True).then_inc(done, 1)
                if layer == 2:
                    pe.wait_ge(main.added, ADDED0 + 3 * TILES)
                    with pe.If(extras > 0):
                        pe.wait_ge(extra.added, ADDED0 + 3 * EXTRAS)
                    for w in range(WINDOWS):
                        if w >= GROUP:
                            pe.wait_ge(s_attended, w - GROUP + 1)
                        pe.transpose(bank[w % GROUP][:, 0:P], S[:, w * P:(w + 1) * P],
                                     ident[:, :]).then_inc(s_back, 1)

        @block.scalar
        def _(act):
            for lane in (main, extra):
                act.sem_inc(lane.hotT, HOTT0)
            act.wait_ge(s_var, 1)
            act.activation(spread[:, :], var[:, :], ACT.Sqrt, bias=eps[:, 0:1]).then_inc(s_root, 1)
            act.wait_ge(s_scale, 1)
            with act.Fori(0, GROUPS) as g:
                for k in range(GROUP):
                    w = ds(g * GROUP + k, 1)
                    act.activation(Hn[:, w, :], X[:, w, :], ACT.Relu, bias=shift[:, w],
                                   scale=rstd[:, w]).then_inc(s_h, 1)
            act.wait_ge(s_var, 2)
            act.activation(spread[:, :], deg[:, 1, :], ACT.Sqrt).then_inc(s_root, 1)
            act.wait_ge(s_steps, 1)
            extras = act.value_load(flags[0:1, 1:2])

            with act.Fori(0, GROUPS) as g:
                for k in range(GROUP):
                    act.wait_ge(s_applied, g * GROUP + (k + 1))
                    at = ds(g * GROUP + k, 1)
                    act.activation(T[:, at, :], T[:, at, :], ACT.Relu, scale=dis[:, at]).then_inc(s_rows, 1)

            def copy_b(w):
                act.wait_ge(s_b, w + 1)
                act.activation(S[:, w * H:(w + 1) * H], bank[B_BANK + w % 2][:, 0:H],
                               ACT.Copy).then_inc(s_bread, 1)

            def root(g, count):
                act.wait_ge(s_var, count + g)
                act.activation(spread[:, span(g)], var[:, span(g)], ACT.Sqrt, bias=eps[:, 0:1]).then_inc(s_root, 1)
                act.wait_ge(s_scale, count - 1 + g)

            for g in range(GROUPS):
                root(g, 3)
                for w in range(g * GROUP, (g + 1) * GROUP + 2):
                    if w < (g + 1) * GROUP:
                        act.activation(Hn[:, w, :], X[:, w, :], ACT.Relu, bias=shift[:, w:w + 1],
                                       scale=rstd[:, w:w + 1]).then_inc(s_h, 1)
                    u = w - 2
                    if u >= g * GROUP:
                        act.wait_ge(s_flip, u + 1)
                        act.activation(hot[:, u % GROUP, :], bank[FLIP + u % 2][:, 0:P],
                                       ACT.Copy).then_inc(s_flipped, 1)
                        if u >= 1:
                            copy_b(u - 1)
            copy_b(WINDOWS - 1)

            def gates(lane_no):
                lane, first, count = LANES[lane_no]

                def copy(i, j):
                    act.wait_ge(lane.turned, i * BLOCK + (j + 1))
                    act.activation(hotT[:, j % 4, :], bank[4 + j % 2][:, 0:P], ACT.Copy).then_inc(lane.hotT, 1)

                def opened(i, j):
                    act.wait_ge(lane.scored, i * BLOCK + (j + SCORED0 + 1))
                    act.activation(gate[:, j % RING:j % RING + 1], score[:, j % RING:j % RING + 1],
                                   ACT.Sigmoid, bias=ab2[:, 0:1]).then_inc(lane.opened, 1)

                def times(i, j):
                    act.wait_ge(lane.opened, i * BLOCK + (j + 1))
                    act.wait_ge(lane.done, i * BLOCK + (2 * count + j + DONE0 - 4 + 1))
                    act.activation(gated[:, j % 4, :], hot[:, j, :], ACT.Copy,
                                   scale=gate[:, j % RING:j % RING + 1]).then_inc(lane.gated, 1)

                sweep(act, count, [(TURN_LAG, copy), (OPEN_LAG, opened), (OPEN_LAG + 1, times)])

            gates(0)
            with act.If(extras > 0):
                gates(1)

            for g in range(GROUPS):
                root(g, 3 + GROUPS)
                for w in of_group(g):
                    act.activation(T[:, w, :], Hn[:, w, :], ACT.Identity, bias=shift[:, w:w + 1],
                                   scale=rstd[:, w:w + 1]).then_inc(s_normed, 1)

        @block.vector
        def _(dve):
            chained = [0]

            def link(ins):
                chained[0] += 1
                ins.then_inc(s_dve, 1)
                dve.wait_ge(s_dve, chained[0])

            for lane in (main, extra):
                dve.sem_inc(lane.added, ADDED0)
                dve.sem_inc(lane.scored, SCORED0)
            dve.memset(dstR[:, FULL, :], N)
            dve.memset(nextR[:, FULL, :], N)
            dve.memset(srcR[:, FULL, :], 0)
            link(dve.memset(wR[:, FULL, :], 0.0))
            dve.drain().then_inc(s_pad, 1)
            dve.memset(eps[:, :], EPS)
            dve.memset(X[:, WINDOWS - 1, :], 0.0).then_inc(s_xpad, 1)

            def col(n):
                return cols[0:ROWS, n, :]

            dve.wait_ge(s_in, 16 * 12)
            dve.wait_ge(s_const, 6)
            link(dve.tensor_tensor(srcF[:, :, :], nextR[:, :, :], dstR[:, :, :], ALU.is_lt))
            link(dve.tensor_reduce(col(VIOLATIONS), srcF[:, :, :], AX.X, ALU.add))
            link(dve.tensor_reduce(cols[0:ROWS, VIOLATIONS, 0:1], col(VIOLATIONS), AX.X, ALU.add))
            dve.drain().then_inc(s_pre, 1)
            dve.wait_ge(s_prep, 1)
            link(dve.tensor_copy(flags[0:1, 0:1], bank[0][0:1, 0:1]))
            dve.drain().then_inc(s_flag, 1)
            disorder = dve.value_load(flags[0:1, 0:1])
            with dve.If(disorder > 0):
                dve.sem_inc(s_sfree, SORT)
                dve.memset(recI[:, :, :], 0)
                dve.drain()
                dve.memset(recI[:, E // P:TILES, 1], N)
                dve.drain().then_inc(s_sclear, 1)
                for digit in range(2):
                    dve.wait_ge(s_sload, 16 * (6 + digit))
                    dve.tensor_scalar(digitI[:, :], recI[:, :, 1], (P - 1, DIGIT)[digit], None,
                                      (ALU.bitwise_and, ALU.logical_shift_right)[digit])
                    dve.drain()
                    dve.tensor_copy(digits[:, :], digitI[:, :])
                    dve.drain()
                    with dve.Fori(0, TILES // SORT) as i:
                        for j in range(SORT):
                            dve.wait_ge(s_scount, i * SORT + (digit * TILES + j + 1))
                            dve.tensor_scalar(hot[:, j, :], iota[:, :], digits[:, ds(i * SORT + j, 1)],
                                              None, ALU.is_equal).then_inc(s_shot, 1)
                    dve.wait_ge(s_stotal, digit + 1)
                    dve.tensor_copy(counts[:, :], bank[0][:, 0:1]).then_inc(s_scounts, 1)
                    dve.wait_ge(s_sstart, digit + 1)
                    dve.tensor_copy(start[:, :], bank[1][0:1, 0:P])
                    dve.tensor_copy(reached[:, :], bank[1][0:1, 0:P])
                    dve.drain().then_inc(s_sstarted, 1)
                    with dve.Fori(0, TILES // SORT) as i:
                        for j in range(SORT):
                            t = i * SORT + j
                            dve.tensor_scalar(hot[:, 8 + j, :], iota[:, :], digits[:, ds(t, 1)],
                                              None, ALU.is_equal).then_inc(s_smark, 1)
                            if j == 0:
                                dve.wait_ge(s_sfree, i * SORT + (digit * TILES + SORT))
                            dve.tensor_copy(moved[:, j, :], recI[:, ds(t, 1), :].rearrange("p t r -> p (t r)"))
                            dve.wait_ge(s_srank, i * SORT + (digit * TILES + j + 1))
                            dve.scalar_tensor_tensor(junk[:, 0, :], bank[2][:, 0:P], 1.0, hot[:, 8 + j, :],
                                                     ALU.mult, ALU.mult, accum_out=placeF[:, 0:1])
                            dve.tensor_copy(reached[:, :], bank[3][0:1, 0:P])
                            dve.drain()
                            dve.tensor_copy(place[:, j:j + 1], placeF[:, :]).then_inc(s_splace, 1)
                dve.wait_ge(s_srows, 16 * 3 * CHUNKS)
            dve.tensor_copy(srcF[:, :, :], srcR[:, :, :])
            link(dve.tensor_copy(dstF[:, :, :], dstR[:, :, :]))
            for k in range(CHUNKS):
                dve.tensor_scalar(localF[:, k, :], dstF[:, k, :], dstF[:, k, 0:1], None, ALU.subtract)
            link(dve.tensor_tensor(spanI[:, 0, :], dstR[:, :, P - 1], dstR[:, :, 0], ALU.subtract))
            link(dve.tensor_scalar(spanI[:, 1, :], spanI[:, 0, :], DIGIT, None, ALU.arith_shift_right))
            link(dve.tensor_copy(col(COUNT), spanI[:, 1, :]))
            dve.drain().then_inc(s_pre, 1)
            dve.wait_ge(s_prep, 3)
            link(dve.tensor_copy(col(TOTAL), bank[2][0:ROWS, 0:CHUNKS]))
            link(dve.tensor_tensor_scan(col(THROUGH), ones[0:ROWS, 0:CHUNKS], col(TOTAL), 0.0, ALU.mult, ALU.add))
            link(dve.tensor_copy(flags[0:1, 1:2], cols[0:1, THROUGH, CHUNKS - 1:CHUNKS]))
            link(dve.tensor_tensor(col(THROUGH), col(THROUGH), col(TOTAL), ALU.subtract))
            link(dve.tensor_tensor(col(UPTO), bank[1][0:ROWS, 0:CHUNKS], col(THROUGH), ALU.add))
            dve.drain().then_inc(s_pre, 1)
            link(dve.tensor_tensor(col(BEFORE), col(UPTO), col(COUNT), ALU.subtract))
            link(dve.tensor_scalar(col(ORIGIN), col(BEFORE), -float(P), float(P), ALU.mult, ALU.add))
            dve.tensor_scalar(col(SHIFT), col(ORIGIN), -1.0, NOWHERE, ALU.mult, ALU.add)
            link(dve.tensor_tensor(col(ORIGIN), col(ORIGIN), dstF[:, :, 0], ALU.add))

            banks4 = 4 * ROWS
            for a, dest in enumerate((srcT, localT, wT, baseF)):
                dve.wait_ge(s_prep, 4 + a)
                lines = 1 if a == 3 else P
                dve.tensor_copy(dest[:, 0:banks4], bank[2 * a][0:lines, 0:banks4])
                last = dve.tensor_copy(dest[:, banks4:TILES], bank[2 * a + 1][0:lines, 0:TILES - banks4])
            link(last)

            for k in range(CHUNKS):
                last = dve.tensor_scalar(chosen[:, k, :], iota[0:ROWS, 0:EXTRAS], cols[0:ROWS, UPTO, k:k + 1],
                                         None, ALU.is_lt)
            link(last)
            for k in range(CHUNKS):
                dve.scalar_tensor_tensor(chosen[:, k, :], iota[0:ROWS, 0:EXTRAS],
                                         cols[0:ROWS, BEFORE, k:k + 1], chosen[:, k, :],
                                         ALU.is_ge, ALU.mult)
                last = dve.tensor_scalar(localF[:, k, :], localF[:, k, :], cols[0:ROWS, SHIFT, k:k + 1],
                                         None, ALU.add)
            link(last)
            dve.drain().then_inc(s_pre, 1)
            dve.wait_ge(s_const, 16)
            dve.tensor_scalar(rowI[:, 1:2], rowI[:, 0:1], PACK - 1, None, ALU.bitwise_and)
            link(dve.tensor_scalar(rowI[:, 2:3], rowI[:, 0:1], 2, 1, ALU.logical_shift_right, ALU.bitwise_and))
            dve.scalar_tensor_tensor(offset[:, :], rowI[:, 1:2], float(WINDOWS + 1), rowI[:, 2:3],
                                     ALU.mult, ALU.add)
            def moments(ws):
                half = stats[:, ws, 0]
                link(dve.tensor_tensor(half, stats[:, ws, 1], stats[:, ws, 4], ALU.subtract))
                dve.tensor_tensor(mean[:, ws], stats[:, ws, 1], stats[:, ws, 4], ALU.add)
                link(dve.scalar_tensor_tensor(half, half, 0.25, half, ALU.mult, ALU.mult))
                dve.tensor_tensor(stats[:, ws, 2], stats[:, ws, 2], stats[:, ws, 5], ALU.add)
                link(dve.tensor_scalar(mean[:, ws], mean[:, ws], 0.5, None, ALU.mult))
                dve.scalar_tensor_tensor(var[:, ws], stats[:, ws, 2], 1.0 / H, half,
                                         ALU.mult, ALU.add).then_inc(s_var, 1)

            def scales(ws, roots):
                dve.wait_ge(s_root, roots)
                link(dve.reciprocal(rstd[:, ws], spread[:, ws]))
                dve.scalar_tensor_tensor(shift[:, ws], mean[:, ws], -1.0, rstd[:, ws],
                                         ALU.mult, ALU.mult).then_inc(s_scale, 1)

            dve.wait_ge(s_x, 32)
            with dve.Fori(0, GROUPS) as g:
                for k in range(GROUP):
                    w = ds(g * GROUP + k, 1)
                    dve.bn_stats(stats[:, w, :], X[:, w, :])
            link(dve.drain())
            moments(slice(0, WINDOWS))

            dve.wait_ge(s_prep, 11)
            dve.tensor_copy(srcT[:, TILES:STEPS], bank[0][:, 0:EXTRAS])
            dve.scalar_tensor_tensor(localT[:, TILES:STEPS], iota[:, 0:EXTRAS], -float(P),
                                     bank[1][:, 0:EXTRAS], ALU.mult, ALU.add)
            dve.tensor_copy(wT[:, TILES:STEPS], bank[2][:, 0:EXTRAS])
            dve.scalar_tensor_tensor(baseF[0:1, TILES:STEPS], iota[0:1, 0:EXTRAS], float(P),
                                     bank[3][0:1, 0:EXTRAS], ALU.mult, ALU.add)
            dve.drain().then_inc(s_dve, 1)
            chained[0] += 1
            dve.wait_ge(s_dve, chained[0])
            dve.sem_inc(s_pre, 1)
            dve.tensor_scalar(localT[:, TILES:STEPS], localT[:, TILES:STEPS], NOWHERE, None, ALU.subtract)
            dve.tensor_copy(baseT[:, :], baseF[:, :])
            dve.drain().then_inc(s_steps, 1)

            scales(slice(0, WINDOWS), 1)

            dve.wait_ge(s_prep, 12)
            for half in range(2):
                at = slice(half * (STEPS // 2), (half + 1) * (STEPS // 2))
                dve.tensor_tensor(stepI[:, 0, at], localT[:, at], bank[6 + half][:, 0:STEPS // 2], ALU.add)
                dve.tensor_copy(stepI[:, 1, at], bank[6 + half][:, 0:STEPS // 2])
            link(dve.scalar_tensor_tensor(own[:, :], localT[:, :], 0.0, wT[:, :], ALU.is_ge, ALU.mult))
            link(dve.tensor_scalar(stepI[:, 1, :], stepI[:, 1, :], DIGIT, None, ALU.logical_shift_right))
            dve.scalar_tensor_tensor(own[:, :], localT[:, :], float(P), own[:, :], ALU.is_lt, ALU.mult)
            dve.tensor_scalar(stripI[:, 0, :], stepI[:, 0, :], STRIP - 1, None, ALU.bitwise_and)
            dve.tensor_tensor(ring1[:, 0:STEPS].rearrange("p (b g t) -> p b g t", g=16, t=PACK),
                              stepI[:, 1, :].rearrange("p (b g t) -> p b g t", g=16, t=PACK),
                              sameGroup[:, :, :].unsqueeze(1).to_broadcast([P, BATCHES, 16, PACK]), ALU.mult)
            link(dve.tensor_scalar(stripI[:, 1, :], stepI[:, 0, :], 5, None, ALU.arith_shift_right))
            dve.scalar_tensor_tensor(strip[:, :], stepI[:, 1, :], -float(PACK), stripI[:, 1, :],
                                     ALU.mult, ALU.add)
            link(dve.tensor_reduce(target[:, :, :], ring1[:, 0:STEPS].rearrange(
                "p (b g t) -> p b t g", g=16, t=PACK), AX.X, ALU.add))
            link(dve.tensor_scalar(target[:, :, :], target[:, :, :], offset[:, 0:1], None, ALU.add))

            def steps_of(a, i, j, wide):
                return a[:, ds(i * (2 * BATCH) + j * BATCH, BATCH)].unsqueeze(2).to_broadcast([P, BATCH, wide])

            def matched(i, j):
                at = stripHot(j).rearrange("p (s r) -> p s r", r=STRIPS)
                dve.tensor_tensor(at, iota[:, 0:STRIPS].unsqueeze(1).to_broadcast([P, BATCH, STRIPS]),
                                  steps_of(strip, i, j, STRIPS), ALU.is_equal).then_inc(s_matched, 1)
                dve.tensor_tensor(placeHot(j).rearrange("p (s r) -> p s r", r=STRIP),
                                  iota[:, 0:STRIP].unsqueeze(1).to_broadcast([P, BATCH, STRIP]),
                                  steps_of(stripI[:, 0, :], i, j, STRIP), ALU.is_equal)
                dve.wait_ge(s_matched, i * 2 + (j + 1))
                dve.tensor_tensor(at, at, steps_of(own, i, j, STRIPS), ALU.mult).then_inc(s_batch, 1)

            def cut(i, j):
                dve.wait_ge(s_crossed, i * 2 + (j + 1))
                dve.tensor_tensor(masked(j).rearrange("p (g s) -> p g s", g=16),
                                  bank[j][:, :].rearrange("p (g s) -> p g s", g=16),
                                  sameStep[:, :, :].rearrange("p t r -> p (t r)").unsqueeze(1).to_broadcast(
                                      [P, 16, PACK * STRIPS]), ALU.mult).then_inc(s_masked, 1)
                dve.wait_ge(s_masked, i * 2 + (j + 1))
                dve.tensor_reduce(sumsOf(j).rearrange("p (g r) -> p g r", r=STRIPS), masked(j).rearrange(
                    "p (g t r) -> p g r t", g=16, t=PACK), AX.X, ALU.add).then_inc(s_cut, 1)

            def ready(i, j):
                dve.wait_ge(s_swapped, i * 2 + (j + 1))
                for t in range(PACK):
                    dve.tensor_scalar(targetHot(j, t), columns[:, :], target[:, ds(i * 2 + j, 1), t],
                                      None, ALU.is_equal)
                dve.tensor_copy(swappedOf(j), bank[2 + j][:, 0:P]).then_inc(s_ready, 1)

            sweep(dve, BATCHES, [(0, matched), (1, cut), (2, ready)], block=2)
            dve.wait_ge(s_strips, 1)
            dve.tensor_copy(strips[:, :], bank[4][0:STRIP, 0:PLACES]).then_inc(s_stacked, 1)
            dve.wait_ge(s_total, 1)
            degree = bank[5][:, 0:WINDOWS]
            link(dve.tensor_scalar(deg[:, 0, :], degree, 0.0, None, ALU.is_gt))
            link(dve.tensor_tensor(deg[:, 1, :], degree, deg[:, 0, :], ALU.mult))
            link(dve.scalar_tensor_tensor(deg[:, 1, :], deg[:, 1, :], 1.0, deg[:, 0, :], ALU.add, ALU.subtract))
            dve.drain().then_inc(s_var, 1)
            dve.wait_ge(s_root, 2)
            link(dve.reciprocal(dis[:, :], spread[:, :]))
            link(dve.tensor_tensor(dis[:, :], dis[:, :], deg[:, 0, :], ALU.mult))

            dve.wait_ge(s_h, WINDOWS)
            for g in range(GROUPS):
                dve.tensor_tensor(T[:, span(g), :], Hn[:, span(g), :],
                                  dis[:, span(g)].unsqueeze(2).to_broadcast([P, GROUP, H]),
                                  ALU.mult).then_inc(s_scaled, 1)
            dve.wait_ge(s_zeroed, 1)
            extras = dve.value_load(flags[0:1, 1:2])

            def sums(layer, lane_no):
                lane, first, count = LANES[lane_no]

                def build(i, j):
                    if j % 4 == 0:
                        dve.wait_ge(lane.done, i * BLOCK + (layer * count + j + 3 + DONE0 - BLOCK + 1))
                    at = ds(i * BLOCK + (first + j), 1)
                    if layer < 2:
                        dve.tensor_scalar(hot[:, j, :], iota[:, :], localT[:, at], wT[:, at],
                                          ALU.is_equal, ALU.mult).then_inc(lane.hot, 1)
                    elif j % AT_ONCE == 0:
                        here = localT[:, ds(i * BLOCK + (first + j), AT_ONCE)]
                        dve.tensor_tensor(hot[:, j:j + AT_ONCE, :],
                                          iota[:, :].unsqueeze(1).to_broadcast([P, AT_ONCE, P]),
                                          here.unsqueeze(2).to_broadcast([P, AT_ONCE, P]),
                                          ALU.is_equal).then_inc(lane.hot, AT_ONCE)

                def scored(i, j):
                    dve.wait_ge(lane.z, i * BLOCK + (j + 1))
                    dve.scalar_tensor_tensor(junk[:, j % 2, :], bank[6 + j % 2][:, 0:H], 0.0, vec[:, 3, :],
                                             ALU.max, ALU.mult, accum_out=score[:, j % RING:j % RING + 1]
                                             ).then_inc(lane.scored, 1)

                bases = []

                def load_bases(i, j):
                    if j % BASES == 0:
                        bases[:] = nc.values_load_multi_w_load_instructions(
                            baseT[0:1, ds(i * BLOCK + (first + j), BASES)], engines=[mybir.EngineType.DVE],
                            min_val=0, max_val=SUMS - P)[1]

                def added(i, j):
                    dve.wait_ge(lane.done, i * BLOCK + (layer * count + j + DONE0 + 1))
                    dve.wait_ge(lane.added, i * BLOCK + (layer * count + j + ADDED0))
                    at = ds(bases[j % BASES], P)
                    dve.tensor_tensor(S[:, at], S[:, at], bank[j % 4][:, 0:P], ALU.add).then_inc(lane.added, 1)

                sweep(dve, count, [(0, build)] + [(SCORE_LAG, scored)] * (layer == 2)
                      + [(ADD_LAG, load_bases), (ADD_LAG, added)])

            for layer in range(3):
                if layer == 2:
                    dve.wait_ge(s_stored[0], 16 * EARLY)
                    dve.memset(S[:, 0:EARLY * GROUP * P], 0.0)
                    dve.wait_ge(s_stored[1], 16 * (GROUPS - EARLY + 1))
                    link(dve.memset(S[:, EARLY * GROUP * P:SUMS], 0.0))
                    link(dve.drain())
                sums(layer, 0)
                with dve.If(extras > 0):
                    dve.wait_ge(main.added, ADDED0 + (layer + 1) * TILES)
                    sums(layer, 1)
                if layer == 0:
                    dve.wait_ge(s_weights, 16 * 10)
                    with dve.Fori(0, GROUPS) as g:
                        for k in range(GROUP):
                            w = g * GROUP + k
                            dve.wait_ge(s_product, w + 1)
                            dve.scalar_tensor_tensor(T[:, ds(w, 1), :], bank[k][:, 0:H], dis[:, ds(w, 1)],
                                                     vec[:, 0, :], ALU.mult, ALU.add).then_inc(s_applied, 1)
                    link(dve.memset(S[:, :], 0.0))
                if layer == 1:
                    dve.wait_ge(s_streamed, 1)
                    for t in range(GROUPS + 3):
                        for w in of_group(t):
                            v, u = w - GROUP, w - 2 * GROUP - 1
                            if t < GROUPS:
                                dve.wait_ge(s_product, WINDOWS + w + 1)
                                dve.scalar_tensor_tensor(T[:, w, :], bank[PRODUCT + w % 2][:, 0:H], dis[:, w:w + 1],
                                                         vec[:, 1, :], ALU.mult, ALU.add).then_inc(s_applied, 1)
                            if 0 <= u < WINDOWS:
                                dve.wait_ge(s_a, u + 1)
                                dve.tensor_tensor(T[:, u, :], bank[A_BANK + u % 2][:, 0:H], vec[:, 2, :],
                                                  ALU.add).then_inc(s_aread, 1)
                            if w > 0 and w <= WINDOWS:
                                dve.wait_ge(s_applied, WINDOWS + w)
                                dve.scalar_tensor_tensor(X[:, w - 1, :], T[:, w - 1, :], 0.0, X[:, w - 1, :],
                                                         ALU.max, ALU.add).then_inc(s_taken, 1)
                            if 1 <= t <= GROUPS:
                                if w % GROUP == 0:
                                    dve.wait_ge(s_taken, w)
                                last = dve.bn_stats(stats[:, v:v + 1, :], X[:, v:v + 1, :])
                        if 1 <= t <= GROUPS:
                            link(last)
                            moments(span(t - 1))
                        if 1 <= t <= GROUPS:
                            scales(span(t - 1), 2 + t)

            for t in range(GROUPS + 1):
                for k in range(GROUP):
                    w, v = t * GROUP + k, (t - 1) * GROUP + k
                    if t < GROUPS:
                        dve.wait_ge(s_back, w + 1)
                        dve.tensor_tensor(Hn[:, w, :], bank[k][:, 0:P], Hn[:, w, :],
                                          ALU.add).then_inc(s_attended, 1)
                    if 1 <= t <= GROUPS:
                        last = dve.bn_stats(stats[:, v:v + 1, :], Hn[:, v:v + 1, :])
                if 1 <= t <= GROUPS:
                    link(last)
                    moments(span(t - 1))
                if 1 <= t <= GROUPS:
                    scales(span(t - 1), 2 + GROUPS + t)
                if t < GROUPS:
                    dve.wait_ge(s_attended, (t + 1) * GROUP)


_INS = ["x", "src", "dst", "edge_weight", "L0_gnn_W1", "L0_gnn_b1", "L0_gnn_W2", "L0_gnn_b2", "L1_gnn_W1",
        "L1_gnn_b1", "L1_gnn_W2", "L1_gnn_b2", "L1_gnn_gamma", "L1_gnn_beta"]


def kernel(**inputs):
    import numpy as np
    import concourse.bacc as bacc
    from concourse import mybir
    from concourse.bass_utils import run_bass_kernel_spmd as run

    nc = bacc.Bacc("TRN2", target_bir_lowering=False, num_devices=1)
    arrays, args = {}, []
    for name in _INS:
        a = np.ascontiguousarray(inputs[name])
        arrays[f"in_{name}"] = a
        args.append(nc.dram_tensor(f"in_{name}", a.shape, mybir.dt.from_np(a.dtype), kind="ExternalInput").ap())
    f32 = mybir.dt.float32
    args.append(nc.dram_tensor("out", (N, H), f32, kind="ExternalOutput").ap())
    for name, shape in (("rows1", (WINDOWS * P, H)), ("rows2", (WINDOWS * P, H)),
                        ("rows3", (WINDOWS * P, 2 * H)), ("brows", (SUMS, H))):
        args.append(nc.dram_tensor(name, shape, f32, kind="Internal").ap())
    args.append(nc.dram_tensor("records", (TILES * P, RECORD), mybir.dt.int32, kind="Internal").ap())
    gnn_kernel(nc, *args)
    r = run(nc, [arrays], core_ids=[0])
    return r.results[0]["out"]
```
